# Optimizing a Trainium2 kernel written in Bass

```python
import numpy as np
import jax
import jax.numpy as jnp

def _softmax(x, axis=-1):
    return jax.nn.softmax(x, axis=axis)
def _gelu(x):
    return jax.nn.gelu(x, approximate=True)
def _silu(x):
    return jax.nn.silu(x)
def _sigmoid(x):
    return jax.nn.sigmoid(x)
def _layernorm(x, axis=-1, eps=1e-5):
    m = jnp.mean(x, axis=axis, keepdims=True)
    v = jnp.var(x, axis=axis, keepdims=True)
    return (x - m) / jnp.sqrt(v + eps)
def _scatter_add(tgt, idx, src, axis=0):
    return tgt.at[idx].add(src)
def _segment_sum(src, seg, n):
    return jax.ops.segment_sum(src, seg, n)

kernel_name = 'mk_conv_preact_d2_conv_nchw256_67e2cb'

def setup_inputs(seed: int = 0):
    np.random.seed(seed)
    _w = jnp.asarray
    def _rec_inputs():
        import jax
        import jax.numpy as jnp
        _gk = jax.random.key(seed)
        x = -7.109e-05 + 0.9999 * jax.random.normal(jax.random.fold_in(_gk, 1), (16, 256, 128, 128), jnp.float32)
        return x
    x = _rec_inputs()
    def _L0_conv_setup():
        import jax, jax.numpy as jnp
        import numpy as np
        DIM_ACTIVE = 64
        C_LL = 16
        EPS = 1e-05

        def _haar_forward(x):
            xe = x[:, :, 0::2, :]
            xo = x[:, :, 1::2, :]
            l = xe + xo
            h = xe - xo
            ll = (l[..., 0::2] + l[..., 1::2]) * 0.5
            lh = (l[..., 0::2] - l[..., 1::2]) * 0.5
            hl = (h[..., 0::2] + h[..., 1::2]) * 0.5
            hh = (h[..., 0::2] - h[..., 1::2]) * 0.5
            return (ll, lh, hl, hh)

        def _ilv_w(a, b):
            return jnp.stack([a, b], axis=-1).reshape(a.shape[:-1] + (a.shape[-1] * 2,))

        def _ilv_h(a, b):
            B, C, Hh, W = a.shape
            return jnp.stack([a, b], axis=3).reshape(B, C, Hh * 2, W)

        def _haar_inverse(ll, lh, hl, hh, H, W):
            l = _ilv_w(ll + lh, ll - lh)
            h = _ilv_w(hl + hh, hl - hh)
            out = _ilv_h(l + h, l - h)
            return out[:, :, :H, :W] * 0.5

        def _dwconv(x, w, pad):
            return jax.lax.conv_general_dilated(x, w, window_strides=(1, 1), padding=pad, dimension_numbers=('NCHW', 'OIHW', 'NCHW'), feature_group_count=x.shape[1])
        key = jax.random.key(seed)
        ks = jax.random.split(key, 8)
        B, C, H, W = (16, 256, 128, 128)
        x = jax.random.normal(ks[0], (B, C, H, W), jnp.float32)
        w_ll = jax.random.normal(ks[1], (C_LL, 1, 3, 3), jnp.float32) * 0.1
        w_lh = jax.random.normal(ks[2], (C_LL, 1, 1, 3), jnp.float32) * 0.1
        w_hl = jax.random.normal(ks[3], (C_LL, 1, 3, 1), jnp.float32) * 0.1
        w_hh = jax.random.normal(ks[4], (C_LL, 1, 3, 3), jnp.float32) * 0.1
        bn_gamma = jnp.ones((C,), jnp.float32)
        bn_beta = jnp.zeros((C,), jnp.float32)
        bn_mean = jax.random.normal(ks[5], (C,), jnp.float32) * 0.1
        bn_var = jax.random.uniform(ks[6], (C,), jnp.float32) * 0.5 + 0.5
        return {'x': x, 'w_ll': w_ll, 'w_lh': w_lh, 'w_hl': w_hl, 'w_hh': w_hh, 'bn_gamma': bn_gamma, 'bn_beta': bn_beta, 'bn_mean': bn_mean, 'bn_var': bn_var}
    _L0_conv_all = _L0_conv_setup()
    _L0_conv_in = {k: v for k, v in _L0_conv_all.items() if k in ('w_ll', 'w_lh', 'w_hl', 'w_hh', 'bn_gamma', 'bn_beta', 'bn_mean', 'bn_var', )}
    del _L0_conv_all

    def _L1_conv_setup():
        import jax, jax.numpy as jnp
        import numpy as np
        IN_DIM, OUT_DIM, BW = (256, 256, 2)
        EPS = 0.001

        def _build_mask_eye(out_dim, in_dim, bw):
            m = np.zeros((out_dim, in_dim), np.float32)
            eye = np.zeros((out_dim, in_dim), np.float32)
            L = min(in_dim, out_dim)
            out_pos = np.linspace(0, out_dim - 1, L)
            in_pos = np.linspace(0, in_dim - 1, L)
            for k in range(L):
                o = int(round(float(out_pos[k])))
                i = int(round(float(in_pos[k])))
                m[max(0, o - bw):min(out_dim - 1, o + bw) + 1, max(0, i - bw):min(in_dim - 1, i + bw) + 1] = 1.0
                eye[o, i] = 1.0
            return (m, eye)
        key = jax.random.key(seed)
        kx, kp = jax.random.split(key)
        x = jax.random.normal(kx, (8, IN_DIM, 256, 256), dtype=jnp.float32)
        P = jax.random.normal(kp, (OUT_DIM, IN_DIM), dtype=jnp.float32)
        m, eye = _build_mask_eye(OUT_DIM, IN_DIM, BW)
        return {'x': x, 'P': P, 'mask': jnp.asarray(m), 'eye': jnp.asarray(eye)}
    _L1_conv_all = _L1_conv_setup()
    _L1_conv_in = {k: v for k, v in _L1_conv_all.items() if k in ('P', 'mask', 'eye', )}
    del _L1_conv_all

    return {
        "x": x,
        "L0_conv_w_ll": _L0_conv_in["w_ll"],
        "L0_conv_w_lh": _L0_conv_in["w_lh"],
        "L0_conv_w_hl": _L0_conv_in["w_hl"],
        "L0_conv_w_hh": _L0_conv_in["w_hh"],
        "L0_conv_bn_gamma": _L0_conv_in["bn_gamma"],
        "L0_conv_bn_beta": _L0_conv_in["bn_beta"],
        "L0_conv_bn_mean": _L0_conv_in["bn_mean"],
        "L0_conv_bn_var": _L0_conv_in["bn_var"],
        "L1_conv_P": _L1_conv_in["P"],
        "L1_conv_mask": _L1_conv_in["mask"],
        "L1_conv_eye": _L1_conv_in["eye"],
    }

def reference(x, L0_conv_w_ll, L0_conv_w_lh, L0_conv_w_hl, L0_conv_w_hh, L0_conv_bn_gamma, L0_conv_bn_beta, L0_conv_bn_mean, L0_conv_bn_var, L1_conv_P, L1_conv_mask, L1_conv_eye):
    import jax
    import jax.numpy as jnp
    def _L0_conv_ref(x, w_ll, w_lh, w_hl, w_hh, bn_gamma, bn_beta, bn_mean, bn_var):
        import jax, jax.numpy as jnp
        import numpy as np
        DIM_ACTIVE = 64
        C_LL = 16
        EPS = 1e-05

        def _haar_forward(x):
            xe = x[:, :, 0::2, :]
            xo = x[:, :, 1::2, :]
            l = xe + xo
            h = xe - xo
            ll = (l[..., 0::2] + l[..., 1::2]) * 0.5
            lh = (l[..., 0::2] - l[..., 1::2]) * 0.5
            hl = (h[..., 0::2] + h[..., 1::2]) * 0.5
            hh = (h[..., 0::2] - h[..., 1::2]) * 0.5
            return (ll, lh, hl, hh)

        def _ilv_w(a, b):
            return jnp.stack([a, b], axis=-1).reshape(a.shape[:-1] + (a.shape[-1] * 2,))

        def _ilv_h(a, b):
            B, C, Hh, W = a.shape
            return jnp.stack([a, b], axis=3).reshape(B, C, Hh * 2, W)

        def _haar_inverse(ll, lh, hl, hh, H, W):
            l = _ilv_w(ll + lh, ll - lh)
            h = _ilv_w(hl + hh, hl - hh)
            out = _ilv_h(l + h, l - h)
            return out[:, :, :H, :W] * 0.5

        def _dwconv(x, w, pad):
            return jax.lax.conv_general_dilated(x, w, window_strides=(1, 1), padding=pad, dimension_numbers=('NCHW', 'OIHW', 'NCHW'), feature_group_count=x.shape[1])
        B, C, H, W = x.shape
        xa = x[:, :DIM_ACTIVE]
        xp = x[:, DIM_ACTIVE:]
        a_ll = xa[:, :C_LL]
        a_lh = xa[:, C_LL:2 * C_LL]
        a_hl = xa[:, 2 * C_LL:3 * C_LL]
        a_hh = xa[:, 3 * C_LL:]
        z = jnp.zeros_like
        ll = _dwconv(_haar_forward(a_ll)[0], w_ll, ((1, 1), (1, 1)))
        p_ll = _haar_inverse(ll, z(ll), z(ll), z(ll), H, W)
        lh = _dwconv(_haar_forward(a_lh)[1], w_lh, ((0, 0), (1, 1)))
        p_lh = _haar_inverse(z(lh), lh, z(lh), z(lh), H, W)
        hl = _dwconv(_haar_forward(a_hl)[2], w_hl, ((1, 1), (0, 0)))
        p_hl = _haar_inverse(z(hl), z(hl), hl, z(hl), H, W)
        hh = _dwconv(_haar_forward(a_hh)[3], w_hh, ((1, 1), (1, 1)))
        p_hh = _haar_inverse(z(hh), z(hh), z(hh), hh, H, W)
        y = jnp.concatenate([p_ll, p_lh, p_hl, p_hh, xp], axis=1)
        inv = jax.lax.rsqrt(bn_var + EPS)
        scale = (bn_gamma * inv)[None, :, None, None]
        shift = (bn_beta - bn_gamma * bn_mean * inv)[None, :, None, None]
        return jax.nn.silu(y * scale + shift)

    def _L1_conv_ref(x, P, mask, eye):
        import jax, jax.numpy as jnp
        import numpy as np
        IN_DIM, OUT_DIM, BW = (256, 256, 2)
        EPS = 0.001

        def _build_mask_eye(out_dim, in_dim, bw):
            m = np.zeros((out_dim, in_dim), np.float32)
            eye = np.zeros((out_dim, in_dim), np.float32)
            L = min(in_dim, out_dim)
            out_pos = np.linspace(0, out_dim - 1, L)
            in_pos = np.linspace(0, in_dim - 1, L)
            for k in range(L):
                o = int(round(float(out_pos[k])))
                i = int(round(float(in_pos[k])))
                m[max(0, o - bw):min(out_dim - 1, o + bw) + 1, max(0, i - bw):min(in_dim - 1, i + bw) + 1] = 1.0
                eye[o, i] = 1.0
            return (m, eye)
        W = jax.nn.softplus(P) * mask + EPS * eye
        return jnp.einsum('oi,bihw->bohw', W, x)

    def _gn(v, G=32, eps=1e-5):
        B_, C_, H_, W_ = v.shape
        g = v.reshape(B_, G, C_ // G, H_, W_)
        m = jnp.mean(g, axis=(2, 3, 4), keepdims=True)
        s = jnp.var(g, axis=(2, 3, 4), keepdims=True)
        return ((g - m) / jnp.sqrt(s + eps)).reshape(v.shape)

    def _ln_c(v, eps=1e-6):
        m = jnp.mean(v, axis=1, keepdims=True)
        s = jnp.var(v, axis=1, keepdims=True)
        return (v - m) / jnp.sqrt(s + eps)

    def _ln_t(v, eps=1e-5):
        m = jnp.mean(v, axis=-1, keepdims=True)
        s = jnp.var(v, axis=-1, keepdims=True)
        return (v - m) / jnp.sqrt(s + eps)

    def _to_tokens(v):
        B_, C_, H_, W_ = v.shape
        return v.reshape(B_, C_, H_ * W_).transpose(0, 2, 1)
    def _from_tokens(t, like):
        B_, C_, H_, W_ = like.shape
        return t.transpose(0, 2, 1).reshape(B_, C_, H_, W_)

    x = x + _L0_conv_ref(_gn(x), L0_conv_w_ll, L0_conv_w_lh, L0_conv_w_hl, L0_conv_w_hh, L0_conv_bn_gamma, L0_conv_bn_beta, L0_conv_bn_mean, L0_conv_bn_var)
    x = x + _L1_conv_ref(_gn(x), L1_conv_P, L1_conv_mask, L1_conv_eye)
    return x


_drawn_inputs = setup_inputs


def setup_inputs(seed=0):
    import zlib

    import numpy as np

    out = dict(_drawn_inputs(seed))
    spreads = {'L0_conv_bn_gamma': (1.0, 0.2), 'L0_conv_bn_beta': (0.0, 0.1)}
    factors = {'L0_conv_w_ll': 2.983, 'L0_conv_w_lh': 4.815, 'L0_conv_w_hl': 4.546, 'L1_conv_eye': 200.0}
    for name, (base, spread) in spreads.items():
        noise = np.random.default_rng([zlib.crc32(name.encode()), seed]).standard_normal(out[name].shape)
        drawn = base * np.exp(spread * noise) if base else spread * noise
        out[name] = jnp.asarray(drawn.astype(out[name].dtype))
    for name, factor in factors.items():
        out[name] = (out[name] * factor).astype(out[name].dtype)
    return out
```

```python
from contextlib import ExitStack

import concourse.bass as bass
import numpy as np
from concourse import mybir

F32 = mybir.dt.float32
BF16 = mybir.dt.bfloat16
I32 = mybir.dt.int32
ALU = mybir.AluOpType
ACT = mybir.ActivationFunctionType
AX = mybir.AxisListType

P = 128
BATCH, CHANNELS, HEIGHT, WIDTH = 16, 256, 128, 128
PIXELS = HEIGHT * WIDTH
ACTIVE = 64
KIND = ACTIVE // 4
ROWS = 8
CHUNK = ROWS * WIDTH
NQ = HEIGHT // ROWS
HALF = CHUNK // 2
GROUP = 8
QROWS, QW = ROWS // 2, WIDTH // 2
BLOCKS = NQ // 2
PAIRS = BLOCKS // 2
BROWS = 2 * QROWS
GN_EPS, BN_EPS, W_EPS = 1e-5, 1e-5, 1e-3
UNROLL = 4
LOOPS = BATCH // UNROLL - 1


ROW_OF = [10, 12, 14] + [1, 3, 5, 7, 9] + [11, 13, 15] + [0, 2, 4, 6, 8]
K_OF = [ROW_OF.index(q) for q in range(NQ)]
T1_ORDER = [k for i in range(5) for k in (3 + i, 11 + i)] + [k for i in range(3) for k in (i, 8 + i)]
SLOTS = 42


def slot(tile, k, image):
    n = image % UNROLL
    if tile == 0:
        if k < 3:
            return k
        if k < 8:
            return 3 + 4 * (k - 3) + n
        if k < 11:
            return 23 + 2 * (k - 8) + n % 2
        return 29 + 2 * (k - 11) + n % 2
    if k < 3:
        return 23 + 2 * k + (n + 1) % 2
    if k < 8:
        return 3 + 4 * (k - 3) + (n - 1) % 4
    if k < 11:
        return 39 + (k - 8)
    return 3 + 4 * (k - 11) + (n - 2) % 4


STATS_A, STATS_B = 4, 12
BN0_AT = [[0, 1, 2, 3], [4, 5, 6, 7], [8, 9, 10], [11, 12, 13], [14, 15]]
HAAR_AT = {0: [0, 1], 1: [2, 3], 2: [4, 5], 3: [6, 7, 8, 9], 4: [10, 11], 5: [12, 13], 6: [14, 15]}
BN1_AT = {5: [0], 6: [1, 2], 7: [3, 4], 8: [5, 6], 9: [7, 8], 10: [9, 10], 11: [11, 12], 12: [13, 14, 15]}
BLOCK_AT = {5 + b: b for b in range(BLOCKS)}
T1_AT = {13: range(0, 5), 14: range(5, 10), 15: range(10, 16)}
ACT_BOTH = 5
SQ_DVE0 = [3, 7, 11, 15]
SQ_DVE1 = [1, 3, 5, 7, 9, 11, 13, 15]
SQ_ACT0 = [q for q in range(NQ) if q not in SQ_DVE0]
SQ_ACT1 = [c for c in range(NQ) if c not in SQ_DVE1]
SQ_ACT = len(SQ_ACT0) + len(SQ_ACT1)


def build(nc, x, P_t, mask_t, eye_t, w_ll, w_lh, w_hl, w_hh, gamma, beta, mean, var, consts, out):
    x_d = x.rearrange("b c h w -> b c (h w)")
    out_d = out.rearrange("b c h w -> b c (h w)")

    nc.disable_value_cache = True
    with ExitStack() as ctx:
        def sb(name, shape, dt=F32):
            return ctx.enter_context(nc.sbuf_tensor(name, shape, dt))

        def sem(name):
            return ctx.enter_context(nc.semaphore(name))

        xs = sb("xs", [P, SLOTS, CHUNK])
        stage = sb("stage", [P, 2, 2, CHUNK])
        wt = sb("wt", [P, 2, CHANNELS])
        lhs = sb("lhs", [P, 2, 2, CHANNELS])
        bias = sb("bias", [P, 2, 2])
        cn = sb("cn", [P, 3 * P + 5])
        lv = sb("lv", [ACTIVE, QROWS, WIDTH])
        cpad = sb("cpad", [P, PAIRS, BROWS + 2, QW + 2])
        prod = sb("prod", [P, 2, BROWS, QW])
        u = sb("u", [P, PAIRS, BROWS, QW])
        junk_a = sb("junk_a", [P, CHUNK], BF16)
        junk_v = sb("junk_v", [P, CHUNK], BF16)
        bnst = sb("bnst", [P, 2, 2 * NQ, 6])
        sums = sb("sums", [P, 2, NQ])
        squares = sb("squares", [P, 2, NQ])
        st = sb("st", [P, 4])
        gs = sb("gs", [P, 4])
        sm = sb("sm", [P, 6, 4])
        rs = sb("rs", [P, 2, 2])
        rs2 = sb("rs2", [P, 2])
        rm2 = sb("rm2", [P, 2])
        pas = sb("pas", [P, 2, 2])
        acts = sb("acts", [P, 5])
        edge = sb("edge", [P, 9])
        edge_m = sb("edge_m", [P, 9])
        pt = sb("pt", [P, 2, 4])
        taps = sb("taps", [P, 9])
        bnp = sb("bnp", [P, 4, 3])
        bns = sb("bns", [P, 4])
        bsh = sb("bsh", [P, 3])

        ident, grp, grp_b = cn[:, 0:P], cn[:, P:2 * P], cn[:, 2 * P:3 * P]
        sign4, ll4 = cn[:, 3 * P:3 * P + 4], cn[:, 3 * P + 4:3 * P + 5]
        sign_h, sign_v = cn[:, 3 * P + 1:3 * P + 2], cn[:, 3 * P + 2:3 * P + 3]

        mm = [ctx.enter_context(nc.psum_tensor(f"mm{m}", [P, CHUNK], F32)) for m in range(2)]
        silu = ctx.enter_context(nc.psum_tensor("silu", [P, 2 * CHUNK], F32))

        x_in = [[sem(f"x{t}_in_{q}") for q in range(NQ)] for t in range(2)]
        params_in = sem("params_in")
        mm_done = sem("mm_done")
        emptied = [sem(f"emptied_{m}") for m in range(2)]
        stored = [[sem(f"stored_{m}_{i}") for i in range(2)] for m in range(2)]
        haar_done = sem("haar_done")
        prod_done = sem("prod_done")
        pair_begun = sem("pair_begun")
        conv_done = sem("conv_done")
        edges_done = sem("edges_done")
        silu0_done = sem("silu0_done")
        silu1_done = sem("silu1_done")
        added = sem("added")
        squared = sem("squared")
        stats_in = sem("stats_in")
        stats_out = sem("stats_out")
        scales_ready = sem("scales_ready")
        lhs_ready = sem("lhs_ready")
        bias_mm = sem("bias_mm")
        bias_ready = sem("bias_ready")
        dve_step = sem("dve_step")
        setup_v = sem("setup_v")
        setup_a = sem("setup_a")
        pads_zero = sem("pads_zero")

        def chunk_of(t, k, image):
            return xs[:, slot(t, k, image), :]

        P_sb = stage[:, 0, 0, 0:512].rearrange("p (t o) -> p t o", t=2)
        mask_sb = stage[:, 0, 0, 512:1024].rearrange("p (t o) -> p t o", t=2)
        eye_sb = stage[:, 0, 1, 0:512].rearrange("p (t o) -> p t o", t=2)
        exp_sb = stage[:, 0, 1, 512:1024].rearrange("p (t o) -> p t o", t=2)
        abs_sb = stage[:, 1, 0, 0:512].rearrange("p (t o) -> p t o", t=2)

        block = ctx.enter_context(nc.Block())

        @block.sync
        def _(sp):
            def load(t, k, image, wrap):
                q = ROW_OF[k]
                sp.dma_start(chunk_of(t, k, wrap), x_d[image, t * P:(t + 1) * P, q * CHUNK:(q + 1) * CHUNK]) \
                    .then_inc(x_in[t][q], 16)

            def param(dst, src):
                sp.dma_start(dst, src, allow_slow_non_contiguous=True).then_inc(params_in, 16)

            def period(n, wrap, more, after):
                for s in range(NQ):
                    if s < 3 or s < 11 and more or s >= 11 and after:
                        if more:
                            sp.wait_ge(mm_done, n * 32 + (2 * s + 2))
                    if more and s < 3:
                        for q in (10 + 2 * s, 11 + 2 * s):
                            load(0, K_OF[q], n + 1, wrap + 1)
                    elif more and s < 11:
                        for i in (2 * (s - 3), 2 * (s - 3) + 1):
                            load(1, T1_ORDER[i], n + 1, wrap + 1)
                    elif after and s >= 11:
                        if s == 11:
                            sp.wait_ge(scales_ready, n * 2 + 3)
                        for q in (2 * (s - 11), 2 * (s - 11) + 1):
                            load(0, K_OF[q], n + 2, wrap + 2)
                    q = ROW_OF[s]
                    for m in range(2):
                        sp.wait_ge(emptied[m], n * NQ + (s + 1))
                        sp.dma_start(out_d[n, m * P:(m + 1) * P, q * CHUNK:(q + 1) * CHUNK],
                                     stage[:, m, s % 2, :]).then_inc(stored[m][s % 2], 16)

            for q in range(4):
                load(0, K_OF[q], 0, 0)
            for j, v in enumerate((gamma, beta, mean, var)):
                column = v.rearrange("(c o) -> c o", o=1)
                param(bnp[:, j, 0:1], column[0:P, :])
                param(bnp[:, j, 1:2], column[P:2 * P, :])
                param(bnp[0:ACTIVE, j, 2:3], column[0:ACTIVE, :])
                param(bnp[ACTIVE:P, j, 2:3], column[0:ACTIVE, :])
            param(cn[:, :], consts)
            sp.wait_ge(setup_v, 1)
            for lane in (0, ACTIVE):
                param(taps[lane:lane + KIND, :], w_ll.rearrange("c o h w -> c (o h w)"))
                param(taps[lane + KIND:lane + 2 * KIND, 3:6], w_lh.rearrange("c o h w -> c (o h w)"))
                param(taps[lane + 2 * KIND:lane + 3 * KIND, 1:8:3], w_hl.rearrange("c o h w -> c (o h w)"))
                param(taps[lane + 3 * KIND:lane + 4 * KIND, :], w_hh.rearrange("c o h w -> c (o h w)"))
            for dst, src in ((P_sb, P_t), (mask_sb, mask_t), (eye_sb, eye_t)):
                param(dst, src.rearrange("(t p) o -> p t o", p=P))
            for q in range(4, NQ):
                load(0, K_OF[q], 0, 0)
            for k in T1_ORDER:
                load(1, k, 0, 0)
            sp.wait_ge(scales_ready, 1)
            for q in range(10):
                load(0, K_OF[q], 1, 1)
            period(0, 0, True, True)
            with sp.Fori(0, LOOPS) as turn:
                for c in range(1, UNROLL + 1):
                    period(sp.snap(turn * UNROLL + c), c, True, True)
            for n in range(LOOPS * UNROLL + 1, BATCH):
                period(n, n % UNROLL, n + 1 < BATCH, n + 2 < BATCH)
            for m in range(2):
                for i in range(2):
                    sp.wait_ge(stored[m][i], 16 * BATCH * NQ // 2)

        PARAMS = 16 * (16 + 1 + 8 + 3)

        @block.tensor
        def _(pe):
            def group_stats(N, event, columns):
                pe.wait_ge(stats_in, N * 3 + (event + 1))
                if event == 0:
                    pe.matmul(silu[:, 2:4], grp_b, st[:, 0:2], start=True, stop=True)
                pe.matmul(silu[:, 0:columns], grp, st[:, 0:columns], start=True, stop=True) \
                    .then_inc(stats_out, 1)

            def layer2_ready(N, wrap):
                group_stats(N, 2, 4)
                pe.wait_ge(lhs_ready, N + 1)
                for m in range(2):
                    for t in range(2):
                        last = pe.matmul(silu[:, m:m + 1], wt[:, t, m * P:(m + 1) * P], rm2[:, t:t + 1],
                                         start=t == 0, stop=t == 1)
                last.then_inc(bias_mm, 1)

            def period(n, wrap, products, prepares):
                N = n + 1
                for s in range(NQ):
                    for m in range(2) if products else ():
                        if not (isinstance(n, int) and n * NQ + s == 0):
                            pe.wait_ge(emptied[m], n * NQ + s)
                        for h in range(2):
                            for t in range(2):
                                last = pe.matmul(mm[m][:, h * HALF:(h + 1) * HALF],
                                                 lhs[:, wrap % 2, t, m * P:(m + 1) * P],
                                                 xs[:, slot(t, s, wrap), h * HALF:(h + 1) * HALF],
                                                 start=t == 0, stop=t == 1)
                        last.then_inc(mm_done, 1)
                    if prepares and s == STATS_A:
                        group_stats(N, 0, 2)
                    if prepares and s == STATS_B:
                        group_stats(N, 1, 2)
                if prepares:
                    layer2_ready(N, wrap + 1)

            period(-1, -1, False, True)
            period(0, 0, True, True)
            with pe.Fori(0, LOOPS) as turn:
                for c in range(1, UNROLL + 1):
                    period(pe.snap(turn * UNROLL + c), c, True, True)
            for n in range(LOOPS * UNROLL + 1, BATCH):
                period(n, n % UNROLL, True, n + 1 < BATCH)

        @block.scalar
        def _(act):
            act.wait_ge(setup_v, 2)
            act.activation(exp_sb, abs_sb, ACT.Exp, scale=-1.0).then_inc(setup_a, 1)
            act.wait_ge(setup_a, 1)
            act.activation(abs_sb, exp_sb, ACT.Ln, bias=1.0).then_inc(setup_a, 1)

            def empty(n, wrap, s, m):
                act.wait_ge(mm_done, n * 32 + (2 * s + m + 1))
                if not (isinstance(n, int) and n == 0 and s < 2):
                    act.wait_ge(stored[m][s % 2], n * 128 + 16 * (s // 2))
                act.activation(stage[:, m, s % 2, :], mm[m][:, :], ACT.Identity,
                               bias=bias[:, wrap % 2, m:m + 1]).then_inc(emptied[m], 1)

            def square(N, wrap, t, i, turn):
                q = i if t == 0 else ROW_OF[T1_ORDER[i]]
                act.wait_ge(added, N * 32 + (16 * t + i + 1))
                if not (isinstance(N, int) and N == 0 and turn == 0):
                    act.wait_ge(squared, N * SQ_ACT + turn)
                act.activation(junk_a[:, :], chunk_of(t, K_OF[q], wrap), ACT.Square,
                               accum_out=squares[:, t, i:i + 1]).then_inc(squared, 1)

            def silu_block(N, wrap, b):
                if b == 0:
                    act.wait_ge(scales_ready, N * 2 + 1)
                else:
                    act.wait_ge(added, N * 32 + 2 * b)
                for j in range(2):
                    act.activation(silu[ACTIVE:P, j * CHUNK:(j + 1) * CHUNK],
                                   xs[ACTIVE:P, slot(0, K_OF[2 * b + j], wrap), :], ACT.Silu,
                                   scale=pas[ACTIVE:P, 0, 0:1], bias=pas[ACTIVE:P, 0, 1:2])
                lane = ACTIVE * (b % 2)
                pixels = silu[0:ACTIVE, :].rearrange("p (i a j b) -> p a b i j", a=2, j=QW, b=2)
                act.wait_ge(edges_done, N * PAIRS + (b // 2 + 1))
                for a in range(2):
                    for c in range(2):
                        j = 2 * a + c
                        last = act.activation(pixels[:, a, c, :, :], u[lane:lane + ACTIVE, b // 2, :, :], ACT.Silu,
                                              scale=acts[lane:lane + ACTIVE, j:j + 1],
                                              bias=acts[lane:lane + ACTIVE, 4:5])
                last.then_inc(silu0_done, 1)

            def silu_chunk(N, wrap, i):
                if i == 0:
                    act.wait_ge(scales_ready, N * 2 + 2)
                elif i >= 2:
                    act.wait_ge(added, N * 32 + (16 + i - 1))
                act.activation(silu[:, (i % 2) * CHUNK:(i % 2 + 1) * CHUNK], chunk_of(1, T1_ORDER[i], wrap), ACT.Silu,
                               scale=pas[:, 1, 0:1], bias=pas[:, 1, 1:2]).then_inc(silu1_done, 1)

            def period(n, wrap, products, prepares):
                N, wrap_n = n + 1, wrap + 1
                turn = 0
                if products:
                    act.wait_ge(bias_ready, n + 1)
                for s in range(NQ):
                    if prepares and s in BLOCK_AT:
                        silu_block(N, wrap_n, BLOCK_AT[s])
                    if prepares and s in T1_AT:
                        for i in T1_AT[s]:
                            silu_chunk(N, wrap_n, i)
                            if i == T1_AT[s][2] and products:
                                empty(n, wrap, s, 0)
                            if i - 2 in SQ_ACT1:
                                square(N, wrap_n, 1, i - 2, turn)
                                turn += 1
                    elif products:
                        empty(n, wrap, s, 0)
                    if products and (s < ACT_BOTH or not prepares):
                        empty(n, wrap, s, 1)
                    if prepares and s - 1 in BLOCK_AT:
                        for q in (2 * BLOCK_AT[s - 1], 2 * BLOCK_AT[s - 1] + 1):
                            if q in SQ_ACT0:
                                square(N, wrap_n, 0, q, turn)
                                turn += 1
                if prepares:
                    for i in (NQ - 2, NQ - 1):
                        if i in SQ_ACT1:
                            square(N, wrap_n, 1, i, turn)
                            turn += 1
                    assert turn == SQ_ACT

            period(-1, -1, False, True)
            period(0, 0, True, True)
            with act.Fori(0, LOOPS) as turn:
                for c in range(1, UNROLL + 1):
                    period(act.snap(turn * UNROLL + c), c, True, True)
            for n in range(LOOPS * UNROLL + 1, BATCH):
                period(n, n % UNROLL, True, n + 1 < BATCH)

        @block.gpsimd
        def _(pool):
            pool.wait_ge(params_in, PARAMS)
            pool.memset(cpad[:, :, :, 0:1], 0.0)
            pool.memset(cpad[:, :, :, QW + 1:QW + 2], 0.0)
            pool.drain()
            pool.memset(cpad[0:ACTIVE, 0, 0, 1:QW + 1], 0.0)
            pool.drain()
            pool.memset(cpad[ACTIVE:P, PAIRS - 1, BROWS + 1, 1:QW + 1], 0.0).then_inc(pads_zero, 1)

            def convolve(N, pb, first):
                if pb == 0 and not first:
                    pool.wait_ge(silu0_done, N * BLOCKS)
                pool.wait_ge(haar_done, N * NQ + min(4 * pb + 5, NQ))
                pool.sem_inc(pair_begun, 1)
                acc = u[:, pb, :, :]
                for tap in range(9):
                    dy, dx = tap // 3, tap % 3
                    c = cpad[:, pb, dy:dy + BROWS, dx:dx + QW]
                    dst = acc if tap == 0 else prod[:, tap % 2, :, :]
                    pool.tensor_scalar(dst, c, taps[:, tap:tap + 1], 0.0, ALU.mult, ALU.add).then_inc(prod_done, 1)
                    if tap:
                        pool.wait_ge(prod_done, N * 9 * PAIRS + (9 * pb + tap + 1))
                        last = pool.tensor_tensor(acc, acc, prod[:, tap % 2, :, :], ALU.add)
                last.then_inc(conv_done, 1)

            for pb in range(PAIRS):
                convolve(0, pb, True)
            with pool.Fori(1, BATCH) as N:
                for pb in range(PAIRS):
                    convolve(N, pb, False)

        @block.vector
        def _(dve):
            def small(chain, last):
                last.then_inc(chain[0], 1)
                chain[2] += 1
                dve.wait_ge(chain[0], chain[1] + chain[2])

            def rsqrt(chain, dst, nv, w, eps):
                a, b, i0, y, hv = (sm[:, j, 0:w] for j in range(1, 6))
                small(chain, dve.tensor_scalar(a, nv, -1.0, eps, ALU.mult, ALU.max))
                dve.tensor_scalar(hv, a, -0.5, None, ALU.mult)
                small(chain, dve.tensor_scalar(i0.bitcast(I32), a.bitcast(I32), 1, None, ALU.logical_shift_right))
                small(chain, dve.tensor_scalar(y.bitcast(I32), i0.bitcast(I32), -1.0, float(0x5F3759DF), ALU.mult, ALU.add))
                for step in range(3):
                    small(chain, dve.tensor_tensor(b, y, y, ALU.mult))
                    small(chain, dve.tensor_tensor(a, b, hv, ALU.mult))
                    small(chain, dve.scalar_tensor_tensor(out=dst if step == 2 else y, in0=a, scalar=1.5, in1=y,
                                                          op0=ALU.add, op1=ALU.mult))

            chain = [setup_v, 0, 0]
            small(chain, dve.memset(taps[:, :], 0.0))
            dve.wait_ge(params_in, PARAMS)
            small(chain, dve.scalar_tensor_tensor(out=abs_sb, in0=P_sb, scalar=-1.0, in1=P_sb, op0=ALU.mult, op1=ALU.max))
            dve.wait_ge(setup_a, 2)
            small(chain, dve.scalar_tensor_tensor(out=exp_sb, in0=P_sb, scalar=0.0, in1=abs_sb, op0=ALU.max, op1=ALU.add))
            small(chain, dve.tensor_tensor(P_sb, exp_sb, mask_sb, ALU.mult))
            small(chain, dve.scalar_tensor_tensor(out=wt[:, :, :], in0=eye_sb, scalar=W_EPS, in1=P_sb, op0=ALU.mult, op1=ALU.add))
            small(chain, dve.tensor_scalar(sm[:, 0, 0:3], bnp[:, 3, :], -1.0, -BN_EPS, ALU.mult, ALU.add))
            rsqrt(chain, sm[:, 0, 0:3], sm[:, 0, 0:3], 3, 0.0)
            small(chain, dve.tensor_tensor(bns[:, 0:3], sm[:, 0, 0:3], bnp[:, 0, :], ALU.mult))
            small(chain, dve.tensor_scalar(bns[:, 3:4], bns[:, 2:3], 0.25, None, ALU.mult))
            small(chain, dve.tensor_tensor(sm[:, 1, 0:3], bns[:, 0:3], bnp[:, 2, :], ALU.mult))
            small(chain, dve.tensor_tensor(bsh[:, :], bnp[:, 1, :], sm[:, 1, 0:3], ALU.subtract))
            by_row = taps[:, :].rearrange("p (y x) -> p y x", y=3)
            by_col = taps[:, :].rearrange("p (y x) -> p x y", y=3)
            small(chain, dve.tensor_reduce(sm[:, 2, 0:3], by_col, AX.X, ALU.add))
            small(chain, dve.tensor_reduce(sm[:, 3, 0:3], by_row, AX.X, ALU.add))
            small(chain, dve.tensor_reduce(sm[:, 4, 0:1], taps[:, :], AX.X, ALU.add))
            small(chain, dve.tensor_scalar(edge[:, 0:2], sm[:, 2, 0:3:2], ll4, None, ALU.mult))
            small(chain, dve.tensor_scalar(edge[:, 2:4], sm[:, 3, 0:3:2], ll4, None, ALU.mult))
            small(chain, dve.tensor_scalar(edge[:, 4:6], taps[:, 0:3:2], ll4, -1.0, ALU.mult, ALU.mult))
            small(chain, dve.tensor_scalar(edge[:, 6:8], taps[:, 6:9:2], ll4, -1.0, ALU.mult, ALU.mult))
            small(chain, dve.tensor_scalar(edge[:, 8:9], sm[:, 4, 0:1], ll4, None, ALU.mult))
            dve.wait_ge(pads_zero, 1)

            def bn(N, wrap, t, i, chain):
                q = i if t == 0 else ROW_OF[T1_ORDER[i]]
                dve.wait_ge(x_in[t][q], N * 16 + 16)
                for h in range(2):
                    last = dve.bn_stats(bnst[:, t, 2 * i + h, :], xs[:, slot(t, K_OF[q], wrap), h * HALF:(h + 1) * HALF])
                last.then_inc(dve_step, 1)
                chain[2] += 1

            def haar(N, wrap, q, chain, first):
                src = xs[0:ACTIVE, slot(0, K_OF[q], wrap), :].rearrange("p (i a w) -> p a i w", a=2, w=WIDTH)
                dve.wait_ge(x_in[0][q], N * 16 + 16)
                if q or not first:
                    dve.wait_ge(haar_done, N * NQ + q)
                l = lv[:, :, :]
                small(chain, dve.scalar_tensor_tensor(out=l, in0=src[:, 1], scalar=sign_v[0:ACTIVE, :], in1=src[:, 0],
                                                      op0=ALU.mult, op1=ALU.add))
                pairs = l.rearrange("p i (j b) -> p b i j", b=2)
                b, row = q // 2, QROWS * (q % 2)
                lane = ACTIVE * (b % 2)

                def across(lane, pb, row, i, rows):
                    return dve.scalar_tensor_tensor(out=cpad[lane:lane + ACTIVE, pb, row:row + rows, 1:QW + 1],
                                                    in0=pairs[:, 1, i:i + rows, :], scalar=sign_h[0:ACTIVE, :],
                                                    in1=pairs[:, 0, i:i + rows, :], op0=ALU.mult, op1=ALU.add)

                if q == 0 and not first:
                    dve.wait_ge(conv_done, N * PAIRS)
                last = across(lane, b // 2, 1 + row, 0, QROWS)
                if q % 2 == 0 and b > 0:
                    last = across(ACTIVE - lane, (b - 1) // 2, BROWS + 1, 0, 1)
                if q % 2 == 1 and b < BLOCKS - 1:
                    last = across(ACTIVE - lane, (b + 1) // 2, 0, QROWS - 1, 1)
                last.then_inc(haar_done, 1)

            def layer1_in(t, chain):
                dve.drain()
                small(chain, dve.bn_aggr(st[:, 0:2], bnst[:, t, :, :].rearrange("p a b -> p (a b)")))
                dve.scalar_tensor_tensor(out=st[:, 1:2], in0=st[:, 0:1], scalar=st[:, 0:1], in1=st[:, 1:2],
                                         op0=ALU.mult, op1=ALU.add).then_inc(stats_in, 1)

            def group_rsqrt(N, event, columns, scale, dst, chain):
                dve.wait_ge(stats_out, N * 3 + (event + 1))
                small(chain, dve.tensor_scalar(gs[:, 0:columns], silu[:, 0:columns], scale, None, ALU.mult))
                m, sq, w = gs[:, 0:columns:2], gs[:, 1:columns:2], columns // 2
                small(chain, dve.tensor_tensor(sm[:, 0, 0:w], m, m, ALU.mult))
                small(chain, dve.scalar_tensor_tensor(out=sm[:, 1, 0:w], in0=sm[:, 0, 0:w], scalar=GN_EPS, in1=sq,
                                                      op0=ALU.subtract, op1=ALU.subtract))
                small(chain, dve.tensor_copy(sm[:, 0, 0:w], sm[:, 1, 0:w]))
                rsqrt(chain, dst, sm[:, 0, 0:w], w, GN_EPS)

            def layer1_out(N, t, chain):
                group_rsqrt(N, t, 4 if t == 0 else 2, 1.0, rs[:, t, 0:2 if t == 0 else 1], chain)
                small(chain, dve.tensor_tensor(pas[:, t, 0:1], rs[:, t, 0:1], bns[:, t:t + 1], ALU.mult))
                if t == 0:
                    dve.tensor_scalar(acts[:, 0:4], sign4, rs[:, 0, 1:2], bns[:, 3:4], ALU.mult, ALU.mult)
                    small(chain, dve.tensor_scalar(edge_m[:, :], edge[:, :], gs[:, 2:3], None, ALU.mult))
                    small(chain, dve.tensor_scalar(pt[:, 0, 0:1], edge_m[:, 8:9], rs[:, 0, 1:2], bns[:, 3:4], ALU.mult, ALU.mult))
                    dve.tensor_tensor(acts[:, 4:5], bsh[:, 2:3], pt[:, 0, 0:1], ALU.subtract)
                small(chain, dve.tensor_tensor(pt[:, t, 1:2], gs[:, 0:1], pas[:, t, 0:1], ALU.mult))
                dve.tensor_tensor(pas[:, t, 1:2], bsh[:, t:t + 1], pt[:, t, 1:2], ALU.subtract).then_inc(scales_ready, 1)

            def edges(N, pb, chain):
                def add(lanes, rows, cols, j):
                    v = u[lanes, pb, rows, cols]
                    return dve.tensor_scalar(v, v, edge_m[lanes, j:j + 1], None, ALU.add)

                dve.wait_ge(conv_done, N * PAIRS + (pb + 1))
                both, low, high = slice(0, P), slice(0, ACTIVE), slice(ACTIVE, P)
                left, right = slice(0, 1), slice(QW - 1, QW)
                add(both, slice(0, BROWS), left, 0)
                last = add(both, slice(0, BROWS), right, 1)
                if pb in (0, PAIRS - 1):
                    lanes, row, j = (low, slice(0, 1), 2) if pb == 0 else (high, slice(BROWS - 1, BROWS), 3)
                    small(chain, last)
                    small(chain, add(lanes, row, slice(0, QW), j))
                    add(lanes, row, left, 4 + 2 * (j - 2))
                    last = add(lanes, row, right, 5 + 2 * (j - 2))
                last.then_inc(edges_done, 1)

            def add_chunk(t, k, wrap, i, buffer):
                x1 = chunk_of(t, k, wrap)
                dve.scalar_tensor_tensor(out=x1, in0=x1, scalar=1.0, in1=silu[:, buffer * CHUNK:(buffer + 1) * CHUNK],
                                         op0=ALU.mult, op1=ALU.add, accum_out=sums[:, t, i:i + 1]).then_inc(added, 1)

            def square(N, wrap, t, i, chain):
                x1 = chunk_of(t, K_OF[i] if t == 0 else T1_ORDER[i], wrap)
                dve.wait_ge(added, N * 32 + (16 * t + i + 1))
                dve.tensor_tensor_reduce(junk_v[:, :], x1, x1, 1.0, 0.0, ALU.mult, ALU.add,
                                         squares[:, t, i:i + 1]).then_inc(dve_step, 1)
                chain[2] += 1

            def empty(n, wrap, s, m):
                dve.wait_ge(mm_done, n * 32 + (2 * s + m + 1))
                if not (isinstance(n, int) and n == 0 and s < 2):
                    dve.wait_ge(stored[m][s % 2], n * 128 + 16 * (s // 2))
                dve.tensor_scalar(stage[:, m, s % 2, :], mm[m][:, :], bias[:, wrap % 2, m:m + 1], None, ALU.add) \
                    .then_inc(emptied[m], 1)

            def layer2(N, wrap, chain):
                dve.wait_ge(dve_step, chain[1] + chain[2])
                dve.wait_ge(added, N * 32 + 32)
                dve.wait_ge(squared, N * SQ_ACT + SQ_ACT)
                dve.tensor_reduce(st[:, 0:4:2], sums[:, :, :], AX.X, ALU.add)
                dve.tensor_reduce(st[:, 1:4:2], squares[:, :, :], AX.X, ALU.add).then_inc(stats_in, 1)
                group_rsqrt(N, 2, 4, 1.0 / PIXELS, rs2[:, :], chain)
                dve.scalar_tensor_tensor(out=rm2[:, :], in0=gs[:, 0:4:2], scalar=-1.0, in1=rs2[:, :], op0=ALU.mult, op1=ALU.mult)
                for t in range(2):
                    own, other = slice(t * P, (t + 1) * P), slice((1 - t) * P, (2 - t) * P)
                    dve.scalar_tensor_tensor(out=lhs[:, wrap % 2, t, own], in0=wt[:, t, own], scalar=rs2[:, t:t + 1],
                                             in1=ident, op0=ALU.mult, op1=ALU.add)
                    last = dve.tensor_scalar(lhs[:, wrap % 2, t, other], wt[:, t, other], rs2[:, t:t + 1], None, ALU.mult)
                last.then_inc(lhs_ready, 1)
                dve.wait_ge(bias_mm, N + 1)
                dve.tensor_copy(bias[:, wrap % 2, :], silu[:, 0:2]).then_inc(bias_ready, 1)

            count = [None]

            def period(n, wrap, products, prepares):
                N, wrap_n = n + 1, wrap + 1
                first = isinstance(n, int) and n < 0
                chain = [dve_step, 0 if first else N * count[0] if prepares else 0, 0]
                for s in range(NQ):
                    if prepares:
                        if s < len(BN0_AT):
                            for q in BN0_AT[s]:
                                bn(N, wrap_n, 0, q, chain)
                        if s == STATS_A:
                            layer1_in(0, chain)
                        for q in HAAR_AT.get(s, ()):
                            haar(N, wrap_n, q, chain, first)
                        if s == STATS_A:
                            layer1_out(N, 0, chain)
                        for i in BN1_AT.get(s, ()):
                            bn(N, wrap_n, 1, i, chain)
                        if s in BLOCK_AT:
                            b = BLOCK_AT[s]
                            if b % 2 == 0:
                                edges(N, b // 2, chain)
                            dve.wait_ge(silu0_done, N * BLOCKS + (b + 1))
                            for j in range(2):
                                q = 2 * b + j
                                add_chunk(0, K_OF[q], wrap_n, q, j)
                                if q in SQ_DVE0:
                                    square(N, wrap_n, 0, q, chain)
                        if s == STATS_B:
                            layer1_in(1, chain)
                            layer1_out(N, 1, chain)
                    emptied_here = not products or not prepares or s < ACT_BOTH
                    for i in T1_AT.get(s, ()) if prepares else ():
                        dve.wait_ge(silu1_done, N * NQ + (i + 1))
                        add_chunk(1, T1_ORDER[i], wrap_n, i, i % 2)
                        if i - 1 in SQ_DVE1:
                            square(N, wrap_n, 1, i - 1, chain)
                        if i == T1_AT[s][2] and not emptied_here:
                            empty(n, wrap, s, 1)
                            emptied_here = True
                    if not emptied_here:
                        empty(n, wrap, s, 1)
                if prepares:
                    if NQ - 1 in SQ_DVE1:
                        square(N, wrap_n, 1, NQ - 1, chain)
                    layer2(N, wrap_n, chain)
                    assert count[0] in (None, chain[2])
                    count[0] = chain[2]

            period(-1, -1, False, True)
            period(0, 0, True, True)
            with dve.Fori(0, LOOPS) as turn:
                for c in range(1, UNROLL + 1):
                    period(dve.snap(turn * UNROLL + c), c, True, True)
            for n in range(LOOPS * UNROLL + 1, BATCH):
                period(n, n % UNROLL, True, n + 1 < BATCH)


def constants():
    p = np.arange(P)
    ident = np.eye(P, dtype=np.float32)
    grp = (p[:, None] // GROUP == p[None, :] // GROUP) / np.float32(GROUP)
    grp_b = (p[:, None] // GROUP == (p[None, :] % ACTIVE) // GROUP) / np.float32(GROUP)
    kind = (p % ACTIVE) // KIND
    sign_h = np.where(kind % 2 == 1, -1.0, 1.0)
    sign_v = np.where(kind >= 2, -1.0, 1.0)
    signs = np.stack([np.ones(P), sign_h, sign_v, sign_h * sign_v], axis=1)
    ll4 = np.where(kind == 0, 4.0, 0.0)[:, None]
    return np.concatenate([ident, grp, grp_b, signs, ll4], axis=1).astype(np.float32)


def kernel(x, L0_conv_w_ll, L0_conv_w_lh, L0_conv_w_hl, L0_conv_w_hh, L0_conv_bn_gamma, L0_conv_bn_beta,
           L0_conv_bn_mean, L0_conv_bn_var, L1_conv_P, L1_conv_mask, L1_conv_eye):
    import concourse.bacc as bacc
    from concourse.bass_utils import run_bass_kernel_spmd

    arrays = {
        "x": x,
        "P_t": np.ascontiguousarray(np.asarray(L1_conv_P).T),
        "mask_t": np.ascontiguousarray(np.asarray(L1_conv_mask).T),
        "eye_t": np.ascontiguousarray(np.asarray(L1_conv_eye).T),
        "w_ll": L0_conv_w_ll, "w_lh": L0_conv_w_lh, "w_hl": L0_conv_w_hl, "w_hh": L0_conv_w_hh,
        "gamma": L0_conv_bn_gamma, "beta": L0_conv_bn_beta, "mean": L0_conv_bn_mean, "var": L0_conv_bn_var,
        "consts": constants(),
    }
    nc = bacc.Bacc("TRN2", target_bir_lowering=False, num_devices=1, dynamic_dma_scratch_size=64)
    ins, feed = [], {}
    for name, a in arrays.items():
        a = np.ascontiguousarray(a)
        feed[f"in_{name}"] = a
        ins.append(nc.dram_tensor(f"in_{name}", a.shape, mybir.dt.from_np(a.dtype), kind="ExternalInput").ap())
    out = nc.dram_tensor("out_x2", (BATCH, CHANNELS, HEIGHT, WIDTH), F32, kind="ExternalOutput").ap()
    build(nc, *ins, out)
    r = run_bass_kernel_spmd(nc, [feed], core_ids=[0])
    return r.results[0]["out_x2"]
```

```python
from contextlib import ExitStack

import concourse.bass as bass
import numpy as np
from concourse import mybir

F32 = mybir.dt.float32
BF16 = mybir.dt.bfloat16
I32 = mybir.dt.int32
ALU = mybir.AluOpType
ACT = mybir.ActivationFunctionType
AX = mybir.AxisListType

P = 128
BATCH, CHANNELS, HEIGHT, WIDTH = 16, 256, 128, 128
PIXELS = HEIGHT * WIDTH
ACTIVE = 64
KIND = ACTIVE // 4
ROWS = 8
CHUNK = ROWS * WIDTH
NQ = HEIGHT // ROWS
HALF = CHUNK // 2
GROUP = 8
QROWS, QW = ROWS // 2, WIDTH // 2
BLOCKS = NQ // 2
PAIRS = BLOCKS // 2
BROWS = 2 * QROWS
CRING, URING = 2, 3
GN_EPS, BN_EPS, W_EPS = 1e-5, 1e-5, 1e-3
UNROLL = 4
LOOPS = BATCH // UNROLL - 1


FIRST = 1
CHAINS = 8 - FIRST
EARLY = 2 * CHAINS
LAST = 8 + FIRST
SLOTS = 4 * FIRST + 6 * CHAINS
K_OF = [k for i in range(CHAINS) for k in (LAST + i, FIRST + i)] + [k for i in range(FIRST) for k in (i, 8 + i)]
ROW_OF = [K_OF.index(k) for k in range(NQ)]
T1_ORDER = [k for i in range(CHAINS) for k in (FIRST + i, LAST + i)] + [k for i in range(FIRST) for k in (i, 8 + i)]


def slot(tile, k, image):
    n = image % UNROLL
    swaps = FIRST + 4 * CHAINS
    if FIRST <= k < 8:
        return FIRST + 4 * (k - FIRST) + (n - tile) % 4
    if k >= LAST:
        return FIRST + 4 * (k - LAST) + (n - 2) % 4 if tile else swaps + 2 * FIRST + 2 * (k - LAST) + n % 2
    if k < FIRST:
        return swaps + 2 * k + (n + 1) % 2 if tile else k
    return swaps + 2 * FIRST + 2 * CHAINS + k - 8 if tile else swaps + 2 * (k - 8) + n % 2


STATS_A, STATS_B = 1, 10
OUT_A = [2]
ACT_BOTH = 2
OUT_BLOCK = [[3], [4], [5], [6], [7], [8], [9], [10]]
OUT_CHUNK = {2: 11, 5: 12, 8: 13, 11: 14, 14: 15}
HAAR_3 = {0: [0], 1: [1], 2: [2], 3: [3], 5: [4], 13: [5], 14: [6], 15: [7]}
HAAR_1 = {5: [8]}
HAAR_A = [9, 10, 11, 12]
HAAR_2 = [[], [], [13, 14, 15], [], [], [], [], []]
BN0_3 = {8: [0], 9: [1], 11: [2], 12: [3]}
BN1_2 = [[0, 1], [2, 3], [4, 5, 6], [7, 8], [9, 10], [11, 12, 13], [14, 15], []]
AHEAD_HAAR = sum(len(v) for v in HAAR_3.values())
AHEAD_BN = sum(len(v) for v in BN0_3.values())
SQ_DVE0 = [1, 5, 9, 13]
SQ_DVE1 = [1, 9]
SQ_ACT0 = [q for q in range(NQ) if q not in SQ_DVE0]
SQ_ACT1 = [c for c in range(NQ) if c not in SQ_DVE1]
SQ_ACT = len(SQ_ACT0) + len(SQ_ACT1)


def build(nc, x, P_t, mask_t, eye_t, w_ll, w_lh, w_hl, w_hh, gamma, beta, mean, var, consts, out):
    x_d = x.rearrange("b c h w -> b c (h w)")
    out_d = out.rearrange("b c h w -> b c (h w)")

    nc.disable_value_cache = True
    with ExitStack() as ctx:
        def sb(name, shape, dt=F32):
            return ctx.enter_context(nc.sbuf_tensor(name, shape, dt))

        def sem(name):
            return ctx.enter_context(nc.semaphore(name))

        xs = sb("xs", [P, SLOTS, CHUNK])
        stage = sb("stage", [P, 2, CHUNK])
        wt = sb("wt", [P, 2, CHANNELS])
        lhs = sb("lhs", [P, 2, CHANNELS])
        bias = sb("bias", [P, 2, 2])
        cn = sb("cn", [P, 3 * P + 5])
        lv = sb("lv", [ACTIVE, 2, QROWS, WIDTH])
        cpad = sb("cpad", [P, CRING, BROWS + 2, QW + 2])
        prod = sb("prod", [P, 2, BROWS, QW])
        u = sb("u", [P, URING, BROWS, QW])
        junk_a = sb("junk_a", [P, CHUNK], BF16)
        junk_v = sb("junk_v", [P, CHUNK], BF16)
        bnst = sb("bnst", [P, 2 * NQ, 6])
        sums = sb("sums", [P, 2, NQ])
        squares = sb("squares", [P, 2, NQ])
        st = sb("st", [P, 4])
        gs = sb("gs", [P, 4])
        sm = sb("sm", [P, 6, 4])
        rs = sb("rs", [P, 2, 2])
        rs2 = sb("rs2", [P, 2])
        rm2 = sb("rm2", [P, 2])
        pas = sb("pas", [P, 2, 2])
        acts = sb("acts", [P, 5])
        edge = sb("edge", [P, 9])
        edge_m = sb("edge_m", [P, 9])
        pt = sb("pt", [P, 2, 4])
        taps = sb("taps", [P, 9])
        bnp = sb("bnp", [P, 4, 3])
        bns = sb("bns", [P, 4])
        bsh = sb("bsh", [P, 3])

        ident, grp, grp_b = cn[:, 0:P], cn[:, P:2 * P], cn[:, 2 * P:3 * P]
        sign4, ll4 = cn[:, 3 * P:3 * P + 4], cn[:, 3 * P + 4:3 * P + 5]
        sign_h, sign_v = cn[:, 3 * P + 1:3 * P + 2], cn[:, 3 * P + 2:3 * P + 3]

        mm = [ctx.enter_context(nc.psum_tensor(f"mm{m}", [P, CHUNK], F32)) for m in range(2)]
        silu = ctx.enter_context(nc.psum_tensor("silu", [P, 2 * CHUNK], F32))

        x_in = [[sem(f"x{t}_in_{q}") for q in range(NQ)] for t in range(2)]
        params_in = sem("params_in")
        mm_done = sem("mm_done")
        emptied = [sem(f"emptied_{m}") for m in range(2)]
        stored = [sem(f"stored_{m}") for m in range(2)]
        lv_done = sem("lv_done")
        haar_done = sem("haar_done")
        prod_done = sem("prod_done")
        pair_begun = sem("pair_begun")
        conv_done = sem("conv_done")
        edges_done = sem("edges_done")
        silu0_done = sem("silu0_done")
        silu1_done = sem("silu1_done")
        added = sem("added")
        squared = sem("squared")
        stats_in = sem("stats_in")
        stats_out = sem("stats_out")
        scales_ready = sem("scales_ready")
        lhs_ready = sem("lhs_ready")
        bias_mm = sem("bias_mm")
        bias_ready = sem("bias_ready")
        dve_step = sem("dve_step")
        setup_v = sem("setup_v")
        setup_a = sem("setup_a")
        pads_zero = sem("pads_zero")

        def chunk_of(t, k, image):
            return xs[:, slot(t, k, image), :]

        P_sb = stage[:, 0, 0:512].rearrange("p (t o) -> p t o", t=2)
        mask_sb = stage[:, 0, 512:1024].rearrange("p (t o) -> p t o", t=2)
        eye_sb = stage[:, 1, 0:512].rearrange("p (t o) -> p t o", t=2)
        exp_sb = stage[:, 1, 512:1024].rearrange("p (t o) -> p t o", t=2)
        abs_sb = u[:, 0, :, :].rearrange("p a b -> p (a b)").rearrange("p (t o) -> p t o", t=2)

        block = ctx.enter_context(nc.Block())

        @block.sync
        def _(sp):
            def load(t, k, image, wrap):
                q = ROW_OF[k]
                sp.dma_start(chunk_of(t, k, wrap), x_d[image, t * P:(t + 1) * P, q * CHUNK:(q + 1) * CHUNK]) \
                    .then_inc(x_in[t][q], 16)

            def param(dst, src):
                sp.dma_start(dst, src, allow_slow_non_contiguous=True).then_inc(params_in, 16)

            def period(n, wrap, more, after):
                def store(s, m):
                    q = ROW_OF[s]
                    sp.wait_ge(emptied[m], n * NQ + (s + 1))
                    sp.dma_start(out_d[n, m * P:(m + 1) * P, q * CHUNK:(q + 1) * CHUNK],
                                 stage[:, m, :]).then_inc(stored[m], 16)

                for s in range(NQ):
                    store(s, 0)
                    if s < LAST and more or s >= LAST and after:
                        sp.wait_ge(mm_done, n * 32 + (2 * s + 2))
                    if s < FIRST and more:
                        for q in (EARLY + 2 * s, EARLY + 2 * s + 1):
                            load(0, K_OF[q], n + 1, wrap + 1)
                    elif s < LAST and more:
                        for i in (2 * (s - FIRST), 2 * (s - FIRST) + 1):
                            load(1, T1_ORDER[i], n + 1, wrap + 1)
                    elif s >= LAST and after:
                        if s == LAST:
                            sp.wait_ge(scales_ready, n * 2 + 3)
                        for q in (2 * (s - LAST), 2 * (s - LAST) + 1):
                            load(0, K_OF[q], n + 2, wrap + 2)
                    store(s, 1)

            for q in range(4):
                load(0, K_OF[q], 0, 0)
            for j, v in enumerate((gamma, beta, mean, var)):
                column = v.rearrange("(c o) -> c o", o=1)
                param(bnp[:, j, 0:1], column[0:P, :])
                param(bnp[:, j, 1:2], column[P:2 * P, :])
                param(bnp[0:ACTIVE, j, 2:3], column[0:ACTIVE, :])
                param(bnp[ACTIVE:P, j, 2:3], column[0:ACTIVE, :])
            param(cn[:, :], consts)
            sp.wait_ge(setup_v, 1)
            for lane in (0, ACTIVE):
                param(taps[lane:lane + KIND, :], w_ll.rearrange("c o h w -> c (o h w)"))
                param(taps[lane + KIND:lane + 2 * KIND, 3:6], w_lh.rearrange("c o h w -> c (o h w)"))
                param(taps[lane + 2 * KIND:lane + 3 * KIND, 1:8:3], w_hl.rearrange("c o h w -> c (o h w)"))
                param(taps[lane + 3 * KIND:lane + 4 * KIND, :], w_hh.rearrange("c o h w -> c (o h w)"))
            for dst, src in ((P_sb, P_t), (mask_sb, mask_t), (eye_sb, eye_t)):
                param(dst, src.rearrange("(t p) o -> p t o", p=P))
            for q in range(4, NQ):
                load(0, K_OF[q], 0, 0)
            for k in T1_ORDER:
                load(1, k, 0, 0)
            sp.wait_ge(scales_ready, 1)
            for q in range(EARLY):
                load(0, K_OF[q], 1, 1)
            period(0, 0, True, True)
            with sp.Fori(0, LOOPS) as turn:
                for c in range(1, UNROLL + 1):
                    period(sp.snap(turn * UNROLL + c), c, True, True)
            for n in range(LOOPS * UNROLL + 1, BATCH):
                period(n, n % UNROLL, n + 1 < BATCH, n + 2 < BATCH)
            for m in range(2):
                sp.wait_ge(stored[m], 16 * BATCH * NQ)

        PARAMS = 16 * (16 + 1 + 8 + 3)
        PRODUCTS = NQ + 9 * PAIRS

        @block.tensor
        def _(pe):
            def group_stats(N, event, columns):
                pe.wait_ge(stats_in, N * 3 + (event + 1))
                if event == 0:
                    pe.matmul(silu[:, 2:4], grp_b, st[:, 0:2], start=True, stop=True)
                pe.matmul(silu[:, 0:columns], grp, st[:, 0:columns], start=True, stop=True) \
                    .then_inc(stats_out, 1)

            def layer2_ready(N, wrap):
                group_stats(N, 2, 4)
                pe.wait_ge(lhs_ready, N * 2 + 1)
                for m in range(2):
                    for t in range(2):
                        last = pe.matmul(silu[:, m:m + 1], wt[:, t, m * P:(m + 1) * P], rm2[:, t:t + 1],
                                         start=t == 0, stop=t == 1)
                last.then_inc(bias_mm, 1)
                pe.wait_ge(lhs_ready, N * 2 + 2)

            def period(n, wrap, products, prepares):
                N = n + 1
                for s in range(NQ):
                    for m in range(2) if products else ():
                        if not (isinstance(n, int) and n * NQ + s == 0):
                            pe.wait_ge(emptied[m], n * NQ + s)
                        for h in range(2):
                            for t in range(2):
                                last = pe.matmul(mm[m][:, h * HALF:(h + 1) * HALF],
                                                 lhs[:, t, m * P:(m + 1) * P],
                                                 xs[:, slot(t, s, wrap), h * HALF:(h + 1) * HALF],
                                                 start=t == 0, stop=t == 1)
                        last.then_inc(mm_done, 1)
                    if prepares and s == STATS_A:
                        group_stats(N, 0, 2)
                    if prepares and s == STATS_B:
                        group_stats(N, 1, 2)
                if prepares:
                    layer2_ready(N, wrap + 1)

            period(-1, -1, False, True)
            period(0, 0, True, True)
            with pe.Fori(0, LOOPS) as turn:
                for c in range(1, UNROLL + 1):
                    period(pe.snap(turn * UNROLL + c), c, True, True)
            for n in range(LOOPS * UNROLL + 1, BATCH):
                period(n, n % UNROLL, True, n + 1 < BATCH)

        @block.scalar
        def _(act):
            act.wait_ge(setup_v, 2)
            act.activation(exp_sb, abs_sb, ACT.Exp, scale=-1.0).then_inc(setup_a, 1)
            act.wait_ge(setup_a, 1)
            act.activation(abs_sb, exp_sb, ACT.Ln, bias=1.0).then_inc(setup_a, 1)

            def empty(n, wrap, s, m):
                act.wait_ge(mm_done, n * 32 + (2 * s + m + 1))
                if not (isinstance(n, int) and n == 0 and s == 0):
                    act.wait_ge(stored[m], n * (16 * NQ) + 16 * s)
                act.activation(stage[:, m, :], mm[m][:, :], ACT.Identity,
                               bias=bias[:, wrap % 2, m:m + 1]).then_inc(emptied[m], 1)

            def square(N, wrap, t, i, turn):
                q = i if t == 0 else ROW_OF[T1_ORDER[i]]
                act.wait_ge(added, N * 32 + (16 * t + i + 1))
                if not (isinstance(N, int) and N == 0 and turn == 0):
                    act.wait_ge(squared, N * SQ_ACT + turn)
                act.activation(junk_a[:, :], chunk_of(t, K_OF[q], wrap), ACT.Square,
                               accum_out=squares[:, t, i:i + 1]).then_inc(squared, 1)

            def silu_block(N, wrap, b):
                if b == 0:
                    act.wait_ge(scales_ready, N * 2 + 1)
                else:
                    act.wait_ge(added, N * 32 + 2 * b)
                for j in range(2):
                    act.activation(silu[ACTIVE:P, j * CHUNK:(j + 1) * CHUNK],
                                   xs[ACTIVE:P, slot(0, K_OF[2 * b + j], wrap), :], ACT.Silu,
                                   scale=pas[ACTIVE:P, 0, 0:1], bias=pas[ACTIVE:P, 0, 1:2])
                lane = ACTIVE * (b % 2)
                pixels = silu[0:ACTIVE, :].rearrange("p (i a j b) -> p a b i j", a=2, j=QW, b=2)
                act.wait_ge(edges_done, N * PAIRS + (b // 2 + 1))
                for a in range(2):
                    for c in range(2):
                        j = 2 * a + c
                        last = act.activation(pixels[:, a, c, :, :], u[lane:lane + ACTIVE, b // 2 % URING, :, :], ACT.Silu,
                                              scale=acts[lane:lane + ACTIVE, j:j + 1],
                                              bias=acts[lane:lane + ACTIVE, 4:5])
                last.then_inc(silu0_done, 1)

            def silu_chunk(N, wrap, i):
                if i == 0:
                    act.wait_ge(scales_ready, N * 2 + 2)
                else:
                    act.wait_ge(added, N * 32 + (16 + i - 1))
                act.activation(silu[:, (i % 2) * CHUNK:(i % 2 + 1) * CHUNK], chunk_of(1, T1_ORDER[i], wrap), ACT.Silu,
                               scale=pas[:, 1, 0:1], bias=pas[:, 1, 1:2]).then_inc(silu1_done, 1)

            def period(n, wrap, products, prepares):
                N, wrap_n = n + 1, wrap + 1
                turn = 0
                if products:
                    act.wait_ge(bias_ready, n + 1)
                if not prepares:
                    for s in range(NQ):
                        empty(n, wrap, s, 0)
                        empty(n, wrap, s, 1)
                    return
                for s in range(ACT_BOTH) if products else ():
                    empty(n, wrap, s, 0)
                    empty(n, wrap, s, 1)
                for s in OUT_A if products else ():
                    empty(n, wrap, s, 0)
                for b in range(BLOCKS):
                    silu_block(N, wrap_n, b)
                    for s in OUT_BLOCK[b] if products else ():
                        empty(n, wrap, s, 0)
                    for q in (2 * b - 2, 2 * b - 1):
                        if q in SQ_ACT0:
                            square(N, wrap_n, 0, q, turn)
                            turn += 1
                for i in range(NQ):
                    if i == 0:
                        for q in (NQ - 2, NQ - 1):
                            if q in SQ_ACT0:
                                square(N, wrap_n, 0, q, turn)
                                turn += 1
                    silu_chunk(N, wrap_n, i)
                    if i in OUT_CHUNK and products:
                        empty(n, wrap, OUT_CHUNK[i], 0)
                    if i - 2 in SQ_ACT1:
                        square(N, wrap_n, 1, i - 2, turn)
                        turn += 1
                for i in (NQ - 2, NQ - 1):
                    if i in SQ_ACT1:
                        square(N, wrap_n, 1, i, turn)
                        turn += 1
                assert turn == SQ_ACT

            period(-1, -1, False, True)
            period(0, 0, True, True)
            with act.Fori(0, LOOPS) as turn:
                for c in range(1, UNROLL + 1):
                    period(act.snap(turn * UNROLL + c), c, True, True)
            for n in range(LOOPS * UNROLL + 1, BATCH):
                period(n, n % UNROLL, True, n + 1 < BATCH)

        @block.gpsimd
        def _(pool):
            pool.wait_ge(params_in, PARAMS)
            pool.memset(cpad[:, :, :, 0:1], 0.0)
            pool.memset(cpad[:, :, :, QW + 1:QW + 2], 0.0).then_inc(pads_zero, 1)

            def convolve(N, pb, first):
                if pb == 0 and not first:
                    pool.wait_ge(silu0_done, N * BLOCKS)
                elif pb >= URING:
                    pool.wait_ge(silu0_done, N * BLOCKS + 2 * (pb - URING + 1))
                pool.wait_ge(haar_done, N * NQ + min(4 * pb + 5, NQ))
                pool.sem_inc(pair_begun, 1)
                acc = u[:, pb % URING, :, :]
                for tap in range(9):
                    dy, dx = tap // 3, tap % 3
                    c = cpad[:, pb % CRING, dy:dy + BROWS, dx:dx + QW]
                    dst = acc if tap == 0 else prod[:, tap % 2, :, :]
                    pool.tensor_scalar(dst, c, taps[:, tap:tap + 1], 0.0, ALU.mult, ALU.add).then_inc(prod_done, 1)
                    if tap:
                        pool.wait_ge(prod_done, N * PRODUCTS + (min(4 * pb + 5, NQ) + 9 * pb + tap + 1))
                        last = pool.tensor_tensor(acc, acc, prod[:, tap % 2, :, :], ALU.add)
                last.then_inc(conv_done, 1)

            def vertical(N, wrap, q, first):
                src = xs[0:ACTIVE, slot(0, K_OF[q], wrap), :].rearrange("p (i a w) -> p a i w", a=2, w=WIDTH)
                l = lv[:, q % 2, :, :]
                pool.wait_ge(x_in[0][q], N * 16 + 16)
                if not first or q >= 2:
                    pool.wait_ge(haar_done, N * NQ + (q - 1))
                pool.sem_inc(pair_begun, 1)
                pool.tensor_scalar(l, src[:, 1], sign_v[0:ACTIVE, :], 0.0, ALU.mult, ALU.add).then_inc(prod_done, 1)
                pool.wait_ge(prod_done, N * PRODUCTS + (q + 1 + 9 * max(0, (q - 1) // 4)))
                pool.tensor_tensor(l, l, src[:, 0], ALU.add).then_inc(lv_done, 1)

            def image(N, wrap, first):
                for q in range(NQ):
                    vertical(N, wrap, q, first)
                    if q % 4 == 0 and q:
                        convolve(N, q // 4 - 1, first)
                convolve(N, PAIRS - 1, first)

            image(0, 0, True)
            image(1, 1, False)
            with pool.Fori(0, LOOPS) as turn:
                for c in range(2, UNROLL + 2):
                    image(pool.snap(turn * UNROLL + c), c, False)
            for n in range(LOOPS * UNROLL + 2, BATCH):
                image(n, n % UNROLL, False)

        @block.vector
        def _(dve):
            def small(chain, last):
                last.then_inc(chain[0], 1)
                chain[2] += 1
                dve.wait_ge(chain[0], chain[1] + chain[2])

            def rsqrt(chain, dst, nv, w, eps):
                a, b, i0, y, hv = (sm[:, j, 0:w] for j in range(1, 6))
                small(chain, dve.tensor_scalar(a, nv, -1.0, eps, ALU.mult, ALU.max))
                dve.tensor_scalar(hv, a, -0.5, None, ALU.mult)
                small(chain, dve.tensor_scalar(i0.bitcast(I32), a.bitcast(I32), 1, None, ALU.logical_shift_right))
                small(chain, dve.tensor_scalar(y.bitcast(I32), i0.bitcast(I32), -1.0, float(0x5F3759DF), ALU.mult, ALU.add))
                for step in range(3):
                    small(chain, dve.tensor_tensor(b, y, y, ALU.mult))
                    small(chain, dve.tensor_tensor(a, b, hv, ALU.mult))
                    small(chain, dve.scalar_tensor_tensor(out=dst if step == 2 else y, in0=a, scalar=1.5, in1=y,
                                                          op0=ALU.add, op1=ALU.mult))

            chain = [setup_v, 0, 0]
            small(chain, dve.memset(taps[:, :], 0.0))
            dve.wait_ge(params_in, PARAMS)
            small(chain, dve.scalar_tensor_tensor(out=abs_sb, in0=P_sb, scalar=-1.0, in1=P_sb, op0=ALU.mult, op1=ALU.max))
            dve.wait_ge(setup_a, 2)
            small(chain, dve.scalar_tensor_tensor(out=exp_sb, in0=P_sb, scalar=0.0, in1=abs_sb, op0=ALU.max, op1=ALU.add))
            small(chain, dve.tensor_tensor(P_sb, exp_sb, mask_sb, ALU.mult))
            small(chain, dve.scalar_tensor_tensor(out=wt[:, :, :], in0=eye_sb, scalar=W_EPS, in1=P_sb, op0=ALU.mult, op1=ALU.add))
            small(chain, dve.tensor_scalar(sm[:, 0, 0:3], bnp[:, 3, :], -1.0, -BN_EPS, ALU.mult, ALU.add))
            rsqrt(chain, sm[:, 0, 0:3], sm[:, 0, 0:3], 3, 0.0)
            small(chain, dve.tensor_tensor(bns[:, 0:3], sm[:, 0, 0:3], bnp[:, 0, :], ALU.mult))
            small(chain, dve.tensor_scalar(bns[:, 3:4], bns[:, 2:3], 0.25, None, ALU.mult))
            small(chain, dve.tensor_tensor(sm[:, 1, 0:3], bns[:, 0:3], bnp[:, 2, :], ALU.mult))
            small(chain, dve.tensor_tensor(bsh[:, :], bnp[:, 1, :], sm[:, 1, 0:3], ALU.subtract))
            by_row = taps[:, :].rearrange("p (y x) -> p y x", y=3)
            by_col = taps[:, :].rearrange("p (y x) -> p x y", y=3)
            small(chain, dve.tensor_reduce(sm[:, 2, 0:3], by_col, AX.X, ALU.add))
            small(chain, dve.tensor_reduce(sm[:, 3, 0:3], by_row, AX.X, ALU.add))
            small(chain, dve.tensor_reduce(sm[:, 4, 0:1], taps[:, :], AX.X, ALU.add))
            small(chain, dve.tensor_scalar(edge[:, 0:2], sm[:, 2, 0:3:2], ll4, None, ALU.mult))
            small(chain, dve.tensor_scalar(edge[:, 2:4], sm[:, 3, 0:3:2], ll4, None, ALU.mult))
            small(chain, dve.tensor_scalar(edge[:, 4:6], taps[:, 0:3:2], ll4, -1.0, ALU.mult, ALU.mult))
            small(chain, dve.tensor_scalar(edge[:, 6:8], taps[:, 6:9:2], ll4, -1.0, ALU.mult, ALU.mult))
            small(chain, dve.tensor_scalar(edge[:, 8:9], sm[:, 4, 0:1], ll4, None, ALU.mult))
            dve.wait_ge(pads_zero, 1)

            def bn(N, wrap, t, i, chain):
                q = i if t == 0 else ROW_OF[T1_ORDER[i]]
                dve.wait_ge(x_in[t][q], N * 16 + 16)
                for h in range(2):
                    last = dve.bn_stats(bnst[:, 2 * i + h, :], xs[:, slot(t, K_OF[q], wrap), h * HALF:(h + 1) * HALF])
                last.then_inc(dve_step, 1)
                chain[2] += 1

            def haar(N, q, first):
                dve.wait_ge(lv_done, N * NQ + (q + 1))
                pairs = lv[:, q % 2, :, :].rearrange("p i (j b) -> p b i j", b=2)
                b, row = q // 2, QROWS * (q % 2)
                lane = ACTIVE * (b % 2)

                def across(lane, pb, row, i, rows):
                    return dve.scalar_tensor_tensor(out=cpad[lane:lane + ACTIVE, pb % CRING, row:row + rows, 1:QW + 1],
                                                    in0=pairs[:, 1, i:i + rows, :], scalar=sign_h[0:ACTIVE, :],
                                                    in1=pairs[:, 0, i:i + rows, :], op0=ALU.mult, op1=ALU.add)

                if q == 0 and not first:
                    dve.wait_ge(conv_done, N * PAIRS)
                elif q >= 4 * CRING - 1 and q % 4 == 3 and q < NQ - 1:
                    dve.wait_ge(conv_done, N * PAIRS + ((q + 1) // 4 - CRING + 1))
                if q == 0:
                    dve.memset(cpad[0:ACTIVE, 0, 0, 1:QW + 1], 0.0)
                if q == NQ - 1:
                    dve.memset(cpad[ACTIVE:P, (PAIRS - 1) % CRING, BROWS + 1, 1:QW + 1], 0.0)
                last = across(lane, b // 2, 1 + row, 0, QROWS)
                if q % 2 == 0 and b > 0:
                    last = across(ACTIVE - lane, (b - 1) // 2, BROWS + 1, 0, 1)
                if q % 2 == 1 and b < BLOCKS - 1:
                    last = across(ACTIVE - lane, (b + 1) // 2, 0, QROWS - 1, 1)
                last.then_inc(haar_done, 1)

            def layer1_in(t, chain):
                dve.drain()
                small(chain, dve.bn_aggr(st[:, 0:2], bnst[:, :, :].rearrange("p a b -> p (a b)")))
                dve.scalar_tensor_tensor(out=st[:, 1:2], in0=st[:, 0:1], scalar=st[:, 0:1], in1=st[:, 1:2],
                                         op0=ALU.mult, op1=ALU.add).then_inc(stats_in, 1)

            def group_rsqrt(N, event, columns, scale, dst, chain):
                dve.wait_ge(stats_out, N * 3 + (event + 1))
                small(chain, dve.tensor_scalar(gs[:, 0:columns], silu[:, 0:columns], scale, None, ALU.mult))
                m, sq, w = gs[:, 0:columns:2], gs[:, 1:columns:2], columns // 2
                small(chain, dve.tensor_tensor(sm[:, 0, 0:w], m, m, ALU.mult))
                small(chain, dve.scalar_tensor_tensor(out=sm[:, 1, 0:w], in0=sm[:, 0, 0:w], scalar=GN_EPS, in1=sq,
                                                      op0=ALU.subtract, op1=ALU.subtract))
                rsqrt(chain, dst, sm[:, 1, 0:w], w, GN_EPS)

            def layer1_out(N, t, chain):
                group_rsqrt(N, t, 4 if t == 0 else 2, 1.0, rs[:, t, 0:2 if t == 0 else 1], chain)
                small(chain, dve.tensor_tensor(pas[:, t, 0:1], rs[:, t, 0:1], bns[:, t:t + 1], ALU.mult))
                if t == 0:
                    dve.tensor_scalar(acts[:, 0:4], sign4, rs[:, 0, 1:2], bns[:, 3:4], ALU.mult, ALU.mult)
                    small(chain, dve.tensor_scalar(edge_m[:, :], edge[:, :], gs[:, 2:3], None, ALU.mult))
                    small(chain, dve.tensor_scalar(pt[:, 0, 0:1], edge_m[:, 8:9], rs[:, 0, 1:2], bns[:, 3:4], ALU.mult, ALU.mult))
                    dve.tensor_tensor(acts[:, 4:5], bsh[:, 2:3], pt[:, 0, 0:1], ALU.subtract)
                small(chain, dve.tensor_tensor(pt[:, t, 1:2], gs[:, 0:1], pas[:, t, 0:1], ALU.mult))
                dve.tensor_tensor(pas[:, t, 1:2], bsh[:, t:t + 1], pt[:, t, 1:2], ALU.subtract).then_inc(scales_ready, 1)

            def edges(N, pb, chain):
                def add(lanes, rows, cols, j):
                    v = u[lanes, pb % URING, rows, cols]
                    return dve.tensor_scalar(v, v, edge_m[lanes, j:j + 1], None, ALU.add)

                dve.wait_ge(conv_done, N * PAIRS + (pb + 1))
                both, low, high = slice(0, P), slice(0, ACTIVE), slice(ACTIVE, P)
                left, right = slice(0, 1), slice(QW - 1, QW)
                add(both, slice(0, BROWS), left, 0)
                last = add(both, slice(0, BROWS), right, 1)
                if pb in (0, PAIRS - 1):
                    lanes, row, j = (low, slice(0, 1), 2) if pb == 0 else (high, slice(BROWS - 1, BROWS), 3)
                    small(chain, last)
                    small(chain, add(lanes, row, slice(0, QW), j))
                    add(lanes, row, left, 4 + 2 * (j - 2))
                    last = add(lanes, row, right, 5 + 2 * (j - 2))
                last.then_inc(edges_done, 1)

            def add_chunk(t, k, wrap, i, buffer):
                x1 = chunk_of(t, k, wrap)
                dve.scalar_tensor_tensor(out=x1, in0=x1, scalar=1.0, in1=silu[:, buffer * CHUNK:(buffer + 1) * CHUNK],
                                         op0=ALU.mult, op1=ALU.add, accum_out=sums[:, t, i:i + 1]).then_inc(added, 1)

            def square(N, wrap, t, i, chain):
                x1 = chunk_of(t, K_OF[i] if t == 0 else T1_ORDER[i], wrap)
                dve.wait_ge(added, N * 32 + (16 * t + i + 1))
                dve.tensor_tensor_reduce(junk_v[:, :], x1, x1, 1.0, 0.0, ALU.mult, ALU.add,
                                         squares[:, t, i:i + 1]).then_inc(dve_step, 1)
                chain[2] += 1

            def empty(n, wrap, s, m):
                dve.wait_ge(mm_done, n * 32 + (2 * s + m + 1))
                dve.wait_ge(stored[m], n * (16 * NQ) + 16 * s)
                dve.tensor_scalar(stage[:, m, :], mm[m][:, :], bias[:, wrap % 2, m:m + 1], None, ALU.add) \
                    .then_inc(emptied[m], 1)

            def layer2(N, wrap, chain):
                dve.wait_ge(dve_step, chain[1] + chain[2])
                dve.wait_ge(added, N * 32 + 32)
                dve.wait_ge(squared, N * SQ_ACT + SQ_ACT)
                dve.tensor_reduce(st[:, 0:4:2], sums[:, :, :], AX.X, ALU.add)
                dve.tensor_reduce(st[:, 1:4:2], squares[:, :, :], AX.X, ALU.add).then_inc(stats_in, 1)
                group_rsqrt(N, 2, 4, 1.0 / PIXELS, rs2[:, :], chain)
                dve.scalar_tensor_tensor(out=rm2[:, :], in0=gs[:, 0:4:2], scalar=-1.0, in1=rs2[:, :], op0=ALU.mult, op1=ALU.mult) \
                    .then_inc(lhs_ready, 1)
                for t in range(2):
                    own, other = slice(t * P, (t + 1) * P), slice((1 - t) * P, (2 - t) * P)
                    dve.scalar_tensor_tensor(out=lhs[:, t, own], in0=wt[:, t, own], scalar=rs2[:, t:t + 1],
                                             in1=ident, op0=ALU.mult, op1=ALU.add)
                    last = dve.tensor_scalar(lhs[:, t, other], wt[:, t, other], rs2[:, t:t + 1], None, ALU.mult)
                last.then_inc(lhs_ready, 1)
                dve.wait_ge(bias_mm, N + 1)
                dve.tensor_copy(bias[:, wrap % 2, :], silu[:, 0:2]).then_inc(bias_ready, 1)

            count = [None]

            def period(n, wrap, products, prepares, after=True):
                if not prepares:
                    return
                N, wrap_n = n + 1, wrap + 1
                first = isinstance(n, int) and n < 0
                if first:
                    chain = [dve_step, 0, 0]
                    for q in range(AHEAD_BN):
                        bn(0, 0, 0, q, chain)
                    for q in range(AHEAD_HAAR):
                        haar(0, q, True)
                chain = [dve_step, AHEAD_BN if first else N * count[0] + AHEAD_BN, 0]
                for q in range(AHEAD_BN, NQ):
                    bn(N, wrap_n, 0, q, chain)
                    for j in HAAR_1.get(q, ()):
                        haar(N, j, first)
                layer1_in(0, chain)
                layer1_out(N, 0, chain)
                edges(N, 0, chain)
                for q in HAAR_A[:2]:
                    haar(N, q, first)
                for s in OUT_A if products else ():
                    empty(n, wrap, s, 1)
                for q in HAAR_A[2:]:
                    haar(N, q, first)
                for b in range(BLOCKS):
                    if b % 2 == 1 and b < BLOCKS - 1:
                        edges(N, b // 2 + 1, chain)
                    dve.wait_ge(silu0_done, N * BLOCKS + (b + 1))
                    for j in range(2):
                        add_chunk(0, K_OF[2 * b + j], wrap_n, 2 * b + j, j)
                    if b == BLOCKS - 1:
                        layer1_in(1, chain)
                        layer1_out(N, 1, chain)
                    for s in OUT_BLOCK[b] if products else ():
                        empty(n, wrap, s, 1)
                    for i in BN1_2[b]:
                        bn(N, wrap_n, 1, i, chain)
                    for j in HAAR_2[b]:
                        haar(N, j, first)
                    for q in (2 * b, 2 * b + 1):
                        if q in SQ_DVE0:
                            square(N, wrap_n, 0, q, chain)
                for i in range(NQ):
                    dve.wait_ge(silu1_done, N * NQ + (i + 1))
                    add_chunk(1, T1_ORDER[i], wrap_n, i, i % 2)
                    if i - 1 in SQ_DVE1:
                        square(N, wrap_n, 1, i - 1, chain)
                    if i in OUT_CHUNK and products:
                        empty(n, wrap, OUT_CHUNK[i], 1)
                    for j in HAAR_3.get(i, ()) if after else ():
                        haar(N + 1, j, False)
                    for q in BN0_3.get(i, ()) if after else ():
                        bn(N + 1, wrap_n + 1, 0, q, chain)
                if NQ - 1 in SQ_DVE1:
                    square(N, wrap_n, 1, NQ - 1, chain)
                layer2(N, wrap_n, chain)
                if not after:
                    return
                assert count[0] in (None, chain[2])
                count[0] = chain[2]

            period(-1, -1, False, True)
            period(0, 0, True, True)
            with dve.Fori(0, LOOPS) as turn:
                for c in range(1, UNROLL + 1):
                    period(dve.snap(turn * UNROLL + c), c, True, True)
            for n in range(LOOPS * UNROLL + 1, BATCH):
                period(n, n % UNROLL, True, n + 1 < BATCH, n + 2 < BATCH)


def constants():
    p = np.arange(P)
    ident = np.eye(P, dtype=np.float32)
    grp = (p[:, None] // GROUP == p[None, :] // GROUP) / np.float32(GROUP)
    grp_b = (p[:, None] // GROUP == (p[None, :] % ACTIVE) // GROUP) / np.float32(GROUP)
    kind = (p % ACTIVE) // KIND
    sign_h = np.where(kind % 2 == 1, -1.0, 1.0)
    sign_v = np.where(kind >= 2, -1.0, 1.0)
    signs = np.stack([np.ones(P), sign_h, sign_v, sign_h * sign_v], axis=1)
    ll4 = np.where(kind == 0, 4.0, 0.0)[:, None]
    return np.concatenate([ident, grp, grp_b, signs, ll4], axis=1).astype(np.float32)


def kernel(x, L0_conv_w_ll, L0_conv_w_lh, L0_conv_w_hl, L0_conv_w_hh, L0_conv_bn_gamma, L0_conv_bn_beta,
           L0_conv_bn_mean, L0_conv_bn_var, L1_conv_P, L1_conv_mask, L1_conv_eye):
    import concourse.bacc as bacc
    from concourse.bass_utils import run_bass_kernel_spmd

    arrays = {
        "x": x,
        "P_t": np.ascontiguousarray(np.asarray(L1_conv_P).T),
        "mask_t": np.ascontiguousarray(np.asarray(L1_conv_mask).T),
        "eye_t": np.ascontiguousarray(np.asarray(L1_conv_eye).T),
        "w_ll": L0_conv_w_ll, "w_lh": L0_conv_w_lh, "w_hl": L0_conv_w_hl, "w_hh": L0_conv_w_hh,
        "gamma": L0_conv_bn_gamma, "beta": L0_conv_bn_beta, "mean": L0_conv_bn_mean, "var": L0_conv_bn_var,
        "consts": constants(),
    }
    nc = bacc.Bacc("TRN2", target_bir_lowering=False, num_devices=1, dynamic_dma_scratch_size=64)
    ins, feed = [], {}
    for name, a in arrays.items():
        a = np.ascontiguousarray(a)
        feed[f"in_{name}"] = a
        ins.append(nc.dram_tensor(f"in_{name}", a.shape, mybir.dt.from_np(a.dtype), kind="ExternalInput").ap())
    out = nc.dram_tensor("out_x2", (BATCH, CHANNELS, HEIGHT, WIDTH), F32, kind="ExternalOutput").ap()
    build(nc, *ins, out)
    r = run_bass_kernel_spmd(nc, [feed], core_ids=[0])
    return r.results[0]["out_x2"]
```

```python
from contextlib import ExitStack

import concourse.bass as bass
import numpy as np
from concourse import mybir

F32 = mybir.dt.float32
BF16 = mybir.dt.bfloat16
I32 = mybir.dt.int32
ALU = mybir.AluOpType
ACT = mybir.ActivationFunctionType
AX = mybir.AxisListType

P = 128
BATCH, CHANNELS, HEIGHT, WIDTH = 16, 256, 128, 128
PIXELS = HEIGHT * WIDTH
ACTIVE = 64
KIND = ACTIVE // 4
ROWS = 8
CHUNK = ROWS * WIDTH
NQ = HEIGHT // ROWS
HALF = CHUNK // 2
GROUP = 8
QROWS, QW = ROWS // 2, WIDTH // 2
BLOCKS = NQ // 2
PAIRS = BLOCKS // 2
BROWS = 2 * QROWS
CRING, URING = 2, 2
GN_EPS, BN_EPS, W_EPS = 1e-5, 1e-5, 1e-3
UNROLL = 4
LOOPS = BATCH // UNROLL - 1


MID = NQ // 2
SLOTS = 6 * MID
K_OF = [k for i in range(MID) for k in (MID + i, i)]
ROW_OF = [K_OF.index(k) for k in range(NQ)]
T1_ORDER = [k for i in range(MID) for k in (i, MID + i)]


def slot(tile, k, image):
    n = image % UNROLL
    if k < MID:
        return 4 * k + (n - tile) % 4
    return 4 * (k - MID) + (n - 2) % 4 if tile else 4 * MID + 2 * (k - MID) + n % 2


STATS_A, STATS_B = (0, 0), (10, 0)
ACT_BOTH = 1
OUT_BLOCK = [[(1, 1)], [(2, 1)], [(3, 0)], [(4, 0), (5, 5)], [(6, 5)], [(7, 3)], [(8, 3)], [(9, 2), (10, 6)]]
OUT_CHUNK = {2: 11, 5: 12, 8: 13, 11: 14, 14: 15}
ACT_CHUNK = {7: 12, 13: 14}
HAAR_3 = {0: [1], 1: [2], 2: [3], 3: [4], 11: [5], 12: [6], 13: [7], 14: [8]}
HAAR_A = [9, 10, 11, 12]
HAAR_2 = [[13, 14], [15], [], [], [], [], [], []]
V_BEFORE = [5, 9, 16, 16]
BN0_3 = {3: [0], 5: [1], 6: [2], 7: [3], 8: [4], 9: [5], 10: [6], 13: [7], 16: [8, 9], 17: [10], 18: [11]}
BN1_2 = [[0, 1, 2], [3, 4], [5, 6], [7, 8], [9, 10], [11, 12], [13, 14, 15], []]
AHEAD_HAAR = 1 + sum(len(v) for v in HAAR_3.values())
AHEAD_BN = sum(len(v) for v in BN0_3.values())
SQ_DVE = {3: 4, 4: 6, 5: 8, 6: 10}
SQ_ACT = 2 * NQ - len(SQ_DVE)


def build(nc, x, P_t, mask_t, eye_t, w_ll, w_lh, w_hl, w_hh, gamma, beta, mean, var, consts, out):
    x_d = x.rearrange("b c h w -> b c (h w)")
    out_d = out.rearrange("b c h w -> b c (h w)")

    nc.disable_value_cache = True
    with ExitStack() as ctx:
        def sb(name, shape, dt=F32):
            return ctx.enter_context(nc.sbuf_tensor(name, shape, dt))

        def sem(name):
            return ctx.enter_context(nc.semaphore(name))

        xs = sb("xs", [P, SLOTS, CHUNK])
        stage = sb("stage", [P, 2, CHUNK])
        wt = sb("wt", [P, 2, CHANNELS])
        lhs = sb("lhs", [P, 2, CHANNELS])
        bias = sb("bias", [P, 2, 2])
        cn = sb("cn", [P, 2 * P + 5])
        lv = sb("lv", [ACTIVE, 2, QROWS, WIDTH])
        cpad = sb("cpad", [P, CRING, BROWS + 2, QW + 2])
        prod = sb("prod", [P, BROWS, QW])
        u = sb("u", [P, URING, BROWS, QW])
        junk = sb("junk", [P, CHUNK], BF16)
        bnst = sb("bnst", [P, 2 * NQ, 6])
        sums = sb("sums", [P, 2, NQ])
        squares = sb("squares", [P, 2, NQ])
        st = sb("st", [P, 4])
        gs = sb("gs", [P, 4])
        sm = sb("sm", [P, 6, 4])
        rs = sb("rs", [P, 2, 2])
        rs2 = sb("rs2", [P, 2])
        rm2 = sb("rm2", [P, 2])
        pas = sb("pas", [P, 2, 2])
        acts = sb("acts", [P, 5])
        edge = sb("edge", [P, 9])
        edge_m = sb("edge_m", [P, 9])
        pt = sb("pt", [P, 2, 4])
        taps = sb("taps", [P, 9])
        bn_folded = sb("bn_folded", [P, 7])
        bns, bsh = bn_folded[:, 0:4], bn_folded[:, 4:7]

        ident, grp = cn[:, 0:P], cn[:, P:2 * P]
        sign4, ll4 = cn[:, 2 * P:2 * P + 4], cn[:, 2 * P + 4:2 * P + 5]
        sign_h, sign_v = cn[:, 2 * P + 1:2 * P + 2], cn[:, 2 * P + 2:2 * P + 3]

        mm = [ctx.enter_context(nc.psum_tensor(f"mm{m}", [P, CHUNK], F32)) for m in range(2)]
        silu = ctx.enter_context(nc.psum_tensor("silu", [P, 2 * CHUNK], F32))

        x_in = [[sem(f"x{t}_in_{q}") for q in range(NQ)] for t in range(2)]
        params_in = sem("params_in")
        mm_done = sem("mm_done")
        emptied = [sem(f"emptied_{m}") for m in range(2)]
        stored = [sem(f"stored_{m}") for m in range(2)]
        lv_done = sem("lv_done")
        haar_done = sem("haar_done")
        prod_done = sem("prod_done")
        pair_begun = sem("pair_begun")
        conv_done = sem("conv_done")
        edges_done = sem("edges_done")
        silu0_done = sem("silu0_done")
        silu1_done = sem("silu1_done")
        added = sem("added")
        squared = sem("squared")
        stats_in = sem("stats_in")
        stats_out = sem("stats_out")
        scales_ready = sem("scales_ready")
        lhs_ready = sem("lhs_ready")
        bias_mm = sem("bias_mm")
        bias_ready = sem("bias_ready")
        dve_step = sem("dve_step")
        setup_v = sem("setup_v")
        setup_a = sem("setup_a")
        pads_zero = sem("pads_zero")

        def chunk_of(t, k, image):
            return xs[:, slot(t, k, image), :]

        bnp = bnst[:, 0:2, :].rearrange("p a b -> p (a b)").rearrange("p (j c) -> p j c", j=4)
        P_sb = stage[:, 0, 0:512].rearrange("p (t o) -> p t o", t=2)
        mask_sb = stage[:, 0, 512:1024].rearrange("p (t o) -> p t o", t=2)
        eye_sb = stage[:, 1, 0:512].rearrange("p (t o) -> p t o", t=2)
        exp_sb = stage[:, 1, 512:1024].rearrange("p (t o) -> p t o", t=2)
        abs_sb = u[:, 0, :, :].rearrange("p a b -> p (a b)").rearrange("p (t o) -> p t o", t=2)

        block = ctx.enter_context(nc.Block())

        @block.sync
        def _(sp):
            def load(t, k, image, wrap):
                q = ROW_OF[k]
                sp.dma_start(chunk_of(t, k, wrap), x_d[image, t * P:(t + 1) * P, q * CHUNK:(q + 1) * CHUNK]) \
                    .then_inc(x_in[t][q], 16)

            def param(dst, src):
                sp.dma_start(dst, src, allow_slow_non_contiguous=True).then_inc(params_in, 16)

            def period(n, wrap, more, after):
                def store(s, m):
                    q = ROW_OF[s]
                    sp.wait_ge(emptied[m], n * NQ + (s + 1))
                    sp.dma_start(out_d[n, m * P:(m + 1) * P, q * CHUNK:(q + 1) * CHUNK],
                                 stage[:, m, :]).then_inc(stored[m], 16)

                for s in range(NQ):
                    store(s, 0)
                    if more if s < MID else after:
                        sp.wait_ge(mm_done, n * 32 + (2 * s + 2))
                    if s < MID and more:
                        for i in (2 * s, 2 * s + 1):
                            load(1, T1_ORDER[i], n + 1, wrap + 1)
                    elif s >= MID and after:
                        if s == MID:
                            sp.wait_ge(scales_ready, n * 2 + 3)
                        for q in (2 * (s - MID), 2 * (s - MID) + 1):
                            load(0, K_OF[q], n + 2, wrap + 2)
                    store(s, 1)

            for q in range(4):
                load(0, K_OF[q], 0, 0)
            for j, v in enumerate((gamma, beta, mean, var)):
                column = v.rearrange("(c o) -> c o", o=1)
                param(bnp[:, j, 0:1], column[0:P, :])
                param(bnp[:, j, 1:2], column[P:2 * P, :])
                param(bnp[0:ACTIVE, j, 2:3], column[0:ACTIVE, :])
                param(bnp[ACTIVE:P, j, 2:3], column[0:ACTIVE, :])
            param(cn[:, :], consts)
            sp.wait_ge(setup_v, 1)
            for lane in (0, ACTIVE):
                param(taps[lane:lane + KIND, :], w_ll.rearrange("c o h w -> c (o h w)"))
                param(taps[lane + KIND:lane + 2 * KIND, 3:6], w_lh.rearrange("c o h w -> c (o h w)"))
                param(taps[lane + 2 * KIND:lane + 3 * KIND, 1:8:3], w_hl.rearrange("c o h w -> c (o h w)"))
                param(taps[lane + 3 * KIND:lane + 4 * KIND, :], w_hh.rearrange("c o h w -> c (o h w)"))
            for dst, src in ((P_sb, P_t), (mask_sb, mask_t), (eye_sb, eye_t)):
                param(dst, src.rearrange("(t p) o -> p t o", p=P))
            for q in range(4, NQ):
                load(0, K_OF[q], 0, 0)
            for k in T1_ORDER:
                load(1, k, 0, 0)
            sp.wait_ge(scales_ready, 1)
            for q in range(NQ):
                load(0, K_OF[q], 1, 1)
            period(0, 0, True, True)
            with sp.Fori(0, LOOPS) as turn:
                for c in range(1, UNROLL + 1):
                    period(sp.snap(turn * UNROLL + c), c, True, True)
            for n in range(LOOPS * UNROLL + 1, BATCH):
                period(n, n % UNROLL, n + 1 < BATCH, n + 2 < BATCH)
            for m in range(2):
                sp.wait_ge(stored[m], 16 * BATCH * NQ)

        PARAMS = 16 * (16 + 1 + 8 + 3)
        PRODUCTS = NQ + 9 * PAIRS

        @block.tensor
        def _(pe):
            def group_stats(N, event, columns):
                pe.wait_ge(stats_in, N * 3 + (event + 1))
                if event == 0:
                    for lane in (0, ACTIVE):
                        pe.matmul(silu[lane:lane + ACTIVE, 2:4], grp[:, 0:ACTIVE], st[:, 0:2], start=True, stop=True)
                pe.matmul(silu[:, 0:columns], grp, st[:, 0:columns], start=True, stop=True) \
                    .then_inc(stats_out, 1)

            def layer2_ready(N, wrap):
                group_stats(N, 2, 4)
                pe.wait_ge(lhs_ready, N * 2 + 1)
                for m in range(2):
                    for t in range(2):
                        last = pe.matmul(silu[:, m:m + 1], wt[:, t, m * P:(m + 1) * P], rm2[:, t:t + 1],
                                         start=t == 0, stop=t == 1)
                last.then_inc(bias_mm, 1)
                pe.wait_ge(lhs_ready, N * 2 + 2)

            def period(n, wrap, products, prepares):
                N = n + 1
                for s in range(NQ):
                    for m in range(2) if products else ():
                        if not (isinstance(n, int) and n * NQ + s == 0):
                            pe.wait_ge(emptied[m], n * NQ + s)
                        for h in range(2):
                            for t in range(2):
                                last = pe.matmul(mm[m][:, h * HALF:(h + 1) * HALF],
                                                 lhs[:, t, m * P:(m + 1) * P],
                                                 xs[:, slot(t, s, wrap), h * HALF:(h + 1) * HALF],
                                                 start=t == 0, stop=t == 1)
                        last.then_inc(mm_done, 1)
                        if prepares and (s, m) == STATS_A:
                            group_stats(N, 0, 2)
                        if prepares and (s, m) == STATS_B:
                            group_stats(N, 1, 2)
                if prepares and not products:
                    group_stats(N, 0, 2)
                    group_stats(N, 1, 2)
                if prepares:
                    layer2_ready(N, wrap + 1)

            period(-1, -1, False, True)
            period(0, 0, True, True)
            with pe.Fori(0, LOOPS) as turn:
                for c in range(1, UNROLL + 1):
                    period(pe.snap(turn * UNROLL + c), c, True, True)
            for n in range(LOOPS * UNROLL + 1, BATCH):
                period(n, n % UNROLL, True, n + 1 < BATCH)

        @block.scalar
        def _(act):
            act.wait_ge(setup_v, 2)
            act.activation(exp_sb, abs_sb, ACT.Exp, scale=-1.0).then_inc(setup_a, 1)
            act.wait_ge(setup_a, 1)
            act.activation(abs_sb, exp_sb, ACT.Ln, bias=1.0).then_inc(setup_a, 1)

            def empty(n, wrap, s, m):
                act.wait_ge(mm_done, n * 32 + (2 * s + m + 1))
                if not (isinstance(n, int) and n == 0 and s == 0):
                    act.wait_ge(stored[m], n * (16 * NQ) + 16 * s)
                act.activation(stage[:, m, :], mm[m][:, :], ACT.Identity,
                               bias=bias[:, wrap % 2, m:m + 1]).then_inc(emptied[m], 1)

            def square(N, wrap, t, i, turn):
                q = i if t == 0 else ROW_OF[T1_ORDER[i]]
                act.wait_ge(added, N * 32 + (16 * t + i + 1))
                if not (isinstance(N, int) and N == 0 and turn == 0):
                    act.wait_ge(squared, N * SQ_ACT + turn)
                act.activation(junk[:, :], chunk_of(t, K_OF[q], wrap), ACT.Square,
                               accum_out=squares[:, t, i:i + 1]).then_inc(squared, 1)

            def silu_block(N, wrap, b, out):
                if b == 0:
                    act.wait_ge(scales_ready, N * 2 + 1)
                else:
                    act.wait_ge(added, N * 32 + 2 * b)
                out(0)
                for j in range(2):
                    act.activation(silu[ACTIVE:P, j * CHUNK:(j + 1) * CHUNK],
                                   xs[ACTIVE:P, slot(0, K_OF[2 * b + j], wrap), :], ACT.Silu,
                                   scale=pas[ACTIVE:P, 0, 0:1], bias=pas[ACTIVE:P, 0, 1:2])
                lane = ACTIVE * (b % 2)
                pixels = silu[0:ACTIVE, :].rearrange("p (i a j b) -> p a b i j", a=2, j=QW, b=2)
                out(1)
                act.wait_ge(edges_done, N * PAIRS + (b // 2 + 1))
                for a in range(2):
                    if a:
                        out(2)
                    for c in range(2):
                        j = 2 * a + c
                        last = act.activation(pixels[:, a, c, :, :], u[lane:lane + ACTIVE, b // 2 % URING, :, :], ACT.Silu,
                                              scale=acts[lane:lane + ACTIVE, j:j + 1],
                                              bias=acts[lane:lane + ACTIVE, 4:5])
                last.then_inc(silu0_done, 1)

            def silu_chunk(N, wrap, i):
                if i == 0:
                    act.wait_ge(scales_ready, N * 2 + 2)
                else:
                    act.wait_ge(added, N * 32 + (16 + i - 1))
                act.activation(silu[:, (i % 2) * CHUNK:(i % 2 + 1) * CHUNK], chunk_of(1, T1_ORDER[i], wrap), ACT.Silu,
                               scale=pas[:, 1, 0:1], bias=pas[:, 1, 1:2]).then_inc(silu1_done, 1)

            def period(n, wrap, products, prepares):
                N, wrap_n = n + 1, wrap + 1
                turn = 0
                if products:
                    act.wait_ge(bias_ready, n + 1)
                if not prepares:
                    for s in range(NQ):
                        empty(n, wrap, s, 0)
                        empty(n, wrap, s, 1)
                    return
                for s in range(ACT_BOTH) if products else ():
                    empty(n, wrap, s, 0)
                    empty(n, wrap, s, 1)
                for b in range(BLOCKS):
                    def out(place):
                        for s, where in OUT_BLOCK[b] if products else ():
                            if where == place:
                                empty(n, wrap, s, 0)

                    silu_block(N, wrap_n, b, out)
                    out(3)
                    for j in range(2):
                        if b and 2 * b - 2 + j not in SQ_DVE.values():
                            square(N, wrap_n, 0, 2 * b - 2 + j, turn)
                            turn += 1
                        out(4 + j)
                for i in range(NQ):
                    if i == 0:
                        for q in (NQ - 2, NQ - 1):
                            square(N, wrap_n, 0, q, turn)
                            turn += 1
                        out(6)
                    silu_chunk(N, wrap_n, i)
                    if i in OUT_CHUNK and products:
                        empty(n, wrap, OUT_CHUNK[i], 0)
                    if i in ACT_CHUNK and products:
                        empty(n, wrap, ACT_CHUNK[i], 1)
                    if i >= 2:
                        square(N, wrap_n, 1, i - 2, turn)
                        turn += 1
                for i in (NQ - 2, NQ - 1):
                    square(N, wrap_n, 1, i, turn)
                    turn += 1
                assert turn == SQ_ACT

            period(-1, -1, False, True)
            period(0, 0, True, True)
            with act.Fori(0, LOOPS) as turn:
                for c in range(1, UNROLL + 1):
                    period(act.snap(turn * UNROLL + c), c, True, True)
            for n in range(LOOPS * UNROLL + 1, BATCH):
                period(n, n % UNROLL, True, n + 1 < BATCH)

        @block.gpsimd
        def _(pool):
            pool.wait_ge(params_in, PARAMS)
            pool.memset(cpad[:, :, :, 0:1], 0.0)
            pool.memset(cpad[:, :, :, QW + 1:QW + 2], 0.0).then_inc(pads_zero, 1)

            def convolve(N, pb, first):
                if pb == 0 and not first:
                    pool.wait_ge(silu0_done, N * BLOCKS)
                elif pb >= URING:
                    pool.wait_ge(silu0_done, N * BLOCKS + 2 * (pb - URING + 1))
                pool.wait_ge(haar_done, N * NQ + min(4 * pb + 5, NQ))
                pool.sem_inc(pair_begun, 1)
                acc = u[:, pb % URING, :, :]
                for tap in range(9):
                    dy, dx = tap // 3, tap % 3
                    c = cpad[:, pb % CRING, dy:dy + BROWS, dx:dx + QW]
                    dst = acc if tap == 0 else prod[:, :, :]
                    if tap:
                        pool.drain()
                    pool.tensor_scalar(dst, c, taps[:, tap:tap + 1], 0.0, ALU.mult, ALU.add).then_inc(prod_done, 1)
                    if tap:
                        pool.wait_ge(prod_done, N * PRODUCTS + (V_BEFORE[pb] + 9 * pb + tap + 1))
                        last = pool.tensor_tensor(acc, acc, prod[:, :, :], ALU.add)
                last.then_inc(conv_done, 1)

            def vertical(N, wrap, q, first):
                src = xs[0:ACTIVE, slot(0, K_OF[q], wrap), :].rearrange("p (i a w) -> p a i w", a=2, w=WIDTH)
                l = lv[:, q % 2, :, :]
                pool.wait_ge(x_in[0][q], N * 16 + 16)
                if not first or q >= 2:
                    pool.wait_ge(haar_done, N * NQ + (q - 1))
                pool.sem_inc(pair_begun, 1)
                pool.tensor_scalar(l, src[:, 1], sign_v[0:ACTIVE, :], 0.0, ALU.mult, ALU.add).then_inc(prod_done, 1)
                pool.wait_ge(prod_done, N * PRODUCTS + (q + 1 + 9 * sum(v <= q for v in V_BEFORE)))
                pool.tensor_tensor(l, l, src[:, 0], ALU.add).then_inc(lv_done, 1)

            def image(N, wrap, first):
                for q in range(NQ + 1):
                    for pb in range(PAIRS):
                        if V_BEFORE[pb] == q:
                            convolve(N, pb, first)
                    if q < NQ:
                        vertical(N, wrap, q, first)

            image(0, 0, True)
            image(1, 1, False)
            with pool.Fori(0, LOOPS) as turn:
                for c in range(2, UNROLL + 2):
                    image(pool.snap(turn * UNROLL + c), c, False)
            for n in range(LOOPS * UNROLL + 2, BATCH):
                image(n, n % UNROLL, False)

        @block.vector
        def _(dve):
            def small(chain, last):
                last.then_inc(chain[0], 1)
                chain[2] += 1
                dve.wait_ge(chain[0], chain[1] + chain[2])

            def rsqrt(chain, dst, nv, w, eps):
                a, b, i0, y, hv = (sm[:, j, 0:w] for j in range(1, 6))
                small(chain, dve.tensor_scalar(a, nv, -1.0, eps, ALU.mult, ALU.max))
                dve.tensor_scalar(hv, a, -0.5, None, ALU.mult)
                small(chain, dve.tensor_scalar(i0.bitcast(I32), a.bitcast(I32), 1, None, ALU.logical_shift_right))
                small(chain, dve.tensor_scalar(y.bitcast(I32), i0.bitcast(I32), -1.0, float(0x5F3759DF), ALU.mult, ALU.add))
                for step in range(3):
                    for c in range(w):
                        last = dve.scalar_tensor_tensor(out=b[:, c:c + 1], in0=y[:, c:c + 1], scalar=y[:, c:c + 1],
                                                        in1=hv[:, c:c + 1], op0=ALU.mult, op1=ALU.mult)
                    small(chain, last)
                    small(chain, dve.scalar_tensor_tensor(out=dst if step == 2 else y, in0=b, scalar=1.5, in1=y,
                                                          op0=ALU.add, op1=ALU.mult))

            chain = [setup_v, 0, 0]
            small(chain, dve.memset(taps[:, :], 0.0))
            dve.wait_ge(params_in, PARAMS)
            small(chain, dve.scalar_tensor_tensor(out=abs_sb, in0=P_sb, scalar=-1.0, in1=P_sb, op0=ALU.mult, op1=ALU.max))
            dve.wait_ge(setup_a, 2)
            small(chain, dve.scalar_tensor_tensor(out=exp_sb, in0=P_sb, scalar=0.0, in1=abs_sb, op0=ALU.max, op1=ALU.add))
            small(chain, dve.tensor_tensor(P_sb, exp_sb, mask_sb, ALU.mult))
            small(chain, dve.scalar_tensor_tensor(out=wt[:, :, :], in0=eye_sb, scalar=W_EPS, in1=P_sb, op0=ALU.mult, op1=ALU.add))
            small(chain, dve.tensor_scalar(sm[:, 0, 0:3], bnp[:, 3, :], -1.0, -BN_EPS, ALU.mult, ALU.add))
            rsqrt(chain, sm[:, 0, 0:3], sm[:, 0, 0:3], 3, 0.0)
            small(chain, dve.tensor_tensor(bns[:, 0:3], sm[:, 0, 0:3], bnp[:, 0, :], ALU.mult))
            small(chain, dve.tensor_scalar(bns[:, 3:4], bns[:, 2:3], 0.25, None, ALU.mult))
            small(chain, dve.tensor_tensor(sm[:, 1, 0:3], bns[:, 0:3], bnp[:, 2, :], ALU.mult))
            small(chain, dve.tensor_tensor(bsh[:, :], bnp[:, 1, :], sm[:, 1, 0:3], ALU.subtract))
            by_row = taps[:, :].rearrange("p (y x) -> p y x", y=3)
            by_col = taps[:, :].rearrange("p (y x) -> p x y", y=3)
            small(chain, dve.tensor_reduce(sm[:, 2, 0:3], by_col, AX.X, ALU.add))
            small(chain, dve.tensor_reduce(sm[:, 3, 0:3], by_row, AX.X, ALU.add))
            small(chain, dve.tensor_reduce(sm[:, 4, 0:1], taps[:, :], AX.X, ALU.add))
            small(chain, dve.tensor_scalar(edge[:, 0:2], sm[:, 2, 0:3:2], ll4, None, ALU.mult))
            small(chain, dve.tensor_scalar(edge[:, 2:4], sm[:, 3, 0:3:2], ll4, None, ALU.mult))
            small(chain, dve.tensor_scalar(edge[:, 4:6], taps[:, 0:3:2], ll4, -1.0, ALU.mult, ALU.mult))
            small(chain, dve.tensor_scalar(edge[:, 6:8], taps[:, 6:9:2], ll4, -1.0, ALU.mult, ALU.mult))
            small(chain, dve.tensor_scalar(edge[:, 8:9], sm[:, 4, 0:1], ll4, None, ALU.mult))
            dve.wait_ge(pads_zero, 1)

            def bn(N, wrap, t, i, chain):
                q = i if t == 0 else ROW_OF[T1_ORDER[i]]
                dve.wait_ge(x_in[t][q], N * 16 + 16)
                for h in range(2):
                    last = dve.bn_stats(bnst[:, 2 * i + h, :], xs[:, slot(t, K_OF[q], wrap), h * HALF:(h + 1) * HALF])
                last.then_inc(dve_step, 1)
                chain[2] += 1

            def haar(N, q, first):
                dve.wait_ge(lv_done, N * NQ + (q + 1))
                pairs = lv[:, q % 2, :, :].rearrange("p i (j b) -> p b i j", b=2)
                b, row = q // 2, QROWS * (q % 2)
                lane = ACTIVE * (b % 2)

                def across(lane, pb, row, i, rows):
                    return dve.scalar_tensor_tensor(out=cpad[lane:lane + ACTIVE, pb % CRING, row:row + rows, 1:QW + 1],
                                                    in0=pairs[:, 1, i:i + rows, :], scalar=sign_h[0:ACTIVE, :],
                                                    in1=pairs[:, 0, i:i + rows, :], op0=ALU.mult, op1=ALU.add)

                if q == 0 and not first:
                    dve.wait_ge(conv_done, N * PAIRS)
                elif q >= 4 * CRING - 1 and q % 4 == 3 and q < NQ - 1:
                    dve.wait_ge(conv_done, N * PAIRS + ((q + 1) // 4 - CRING + 1))
                if q == 0:
                    dve.memset(cpad[0:ACTIVE, 0, 0, 1:QW + 1], 0.0)
                if q == NQ - 1:
                    dve.memset(cpad[ACTIVE:P, (PAIRS - 1) % CRING, BROWS + 1, 1:QW + 1], 0.0)
                last = across(lane, b // 2, 1 + row, 0, QROWS)
                if q % 2 == 0 and b > 0:
                    last = across(ACTIVE - lane, (b - 1) // 2, BROWS + 1, 0, 1)
                if q % 2 == 1 and b < BLOCKS - 1:
                    last = across(ACTIVE - lane, (b + 1) // 2, 0, QROWS - 1, 1)
                last.then_inc(haar_done, 1)

            def layer1_in(t, chain):
                dve.drain()
                small(chain, dve.bn_aggr(st[:, 0:2], bnst[:, :, :].rearrange("p a b -> p (a b)")))
                dve.scalar_tensor_tensor(out=st[:, 1:2], in0=st[:, 0:1], scalar=st[:, 0:1], in1=st[:, 1:2],
                                         op0=ALU.mult, op1=ALU.add).then_inc(stats_in, 1)

            def group_rsqrt(N, event, columns, scale, dst, chain, early=lambda: None):
                dve.wait_ge(stats_out, N * 3 + (event + 1))
                small(chain, dve.tensor_scalar(gs[:, 0:columns], silu[:, 0:columns], scale, None, ALU.mult))
                early()
                m, sq, w = gs[:, 0:columns:2], gs[:, 1:columns:2], columns // 2
                small(chain, dve.tensor_tensor(sm[:, 0, 0:w], m, m, ALU.mult))
                small(chain, dve.scalar_tensor_tensor(out=sm[:, 1, 0:w], in0=sm[:, 0, 0:w], scalar=GN_EPS, in1=sq,
                                                      op0=ALU.subtract, op1=ALU.subtract))
                rsqrt(chain, dst, sm[:, 1, 0:w], w, GN_EPS)

            def layer1_out(N, t, chain):
                def early():
                    if t == 0:
                        dve.tensor_scalar(edge_m[:, :], edge[:, :], gs[:, 2:3], None, ALU.mult)

                group_rsqrt(N, t, 4 if t == 0 else 2, 1.0, rs[:, t, 0:2 if t == 0 else 1], chain, early)
                if t == 0:
                    dve.tensor_scalar(acts[:, 0:4], sign4, rs[:, 0, 1:2], bns[:, 3:4], ALU.mult, ALU.mult)
                    dve.tensor_scalar(pt[:, 0, 0:1], edge_m[:, 8:9], rs[:, 0, 1:2], bns[:, 3:4], ALU.mult, ALU.mult)
                small(chain, dve.tensor_tensor(pas[:, t, 0:1], rs[:, t, 0:1], bns[:, t:t + 1], ALU.mult))
                if t == 0:
                    dve.tensor_tensor(acts[:, 4:5], bsh[:, 2:3], pt[:, 0, 0:1], ALU.subtract)
                small(chain, dve.tensor_tensor(pt[:, t, 1:2], gs[:, 0:1], pas[:, t, 0:1], ALU.mult))
                dve.tensor_tensor(pas[:, t, 1:2], bsh[:, t:t + 1], pt[:, t, 1:2], ALU.subtract).then_inc(scales_ready, 1)

            def edges(N, pb, chain):
                def add(lanes, rows, cols, j):
                    v = u[lanes, pb % URING, rows, cols]
                    return dve.tensor_scalar(v, v, edge_m[lanes, j:j + 1], None, ALU.add)

                dve.wait_ge(conv_done, N * PAIRS + (pb + 1))
                both, low, high = slice(0, P), slice(0, ACTIVE), slice(ACTIVE, P)
                left, right = slice(0, 1), slice(QW - 1, QW)
                add(both, slice(0, BROWS), left, 0)
                last = add(both, slice(0, BROWS), right, 1)
                if pb in (0, PAIRS - 1):
                    lanes, row, j = (low, slice(0, 1), 2) if pb == 0 else (high, slice(BROWS - 1, BROWS), 3)
                    small(chain, last)
                    small(chain, add(lanes, row, slice(0, QW), j))
                    add(lanes, row, left, 4 + 2 * (j - 2))
                    last = add(lanes, row, right, 5 + 2 * (j - 2))
                last.then_inc(edges_done, 1)

            def add_chunk(t, k, wrap, i, buffer):
                x1 = chunk_of(t, k, wrap)
                dve.scalar_tensor_tensor(out=x1, in0=x1, scalar=1.0, in1=silu[:, buffer * CHUNK:(buffer + 1) * CHUNK],
                                         op0=ALU.mult, op1=ALU.add, accum_out=sums[:, t, i:i + 1]).then_inc(added, 1)

            def square(n, N, wrap, q, s, chain):
                if n is not None:
                    dve.wait_ge(stored[1], n * (16 * NQ) + 16 * s)
                dve.wait_ge(added, N * 32 + (q + 1))
                x1 = chunk_of(0, K_OF[q], wrap)
                small(chain, dve.tensor_tensor_reduce(stage[:, 1, :], x1, x1, 1.0, 0.0, ALU.mult, ALU.add,
                                                      squares[:, 0, q:q + 1]))

            def empty(n, wrap, s, m):
                dve.wait_ge(mm_done, n * 32 + (2 * s + m + 1))
                dve.wait_ge(stored[m], n * (16 * NQ) + 16 * s)
                dve.tensor_scalar(stage[:, m, :], mm[m][:, :], bias[:, wrap % 2, m:m + 1], None, ALU.add) \
                    .then_inc(emptied[m], 1)

            def layer2(N, wrap, chain, ahead):
                dve.wait_ge(dve_step, chain[1] + chain[2])
                dve.wait_ge(added, N * 32 + 32)
                dve.wait_ge(squared, N * SQ_ACT + SQ_ACT)
                dve.tensor_reduce(st[:, 0:4:2], sums[:, :, :], AX.X, ALU.add)
                dve.tensor_reduce(st[:, 1:4:2], squares[:, :, :], AX.X, ALU.add).then_inc(stats_in, 1)
                ahead(NQ + 1)
                group_rsqrt(N, 2, 4, 1.0 / PIXELS, rs2[:, :], chain)
                dve.scalar_tensor_tensor(out=rm2[:, :], in0=gs[:, 0:4:2], scalar=-1.0, in1=rs2[:, :], op0=ALU.mult, op1=ALU.mult) \
                    .then_inc(lhs_ready, 1)
                for t in range(2):
                    own, other = slice(t * P, (t + 1) * P), slice((1 - t) * P, (2 - t) * P)
                    dve.scalar_tensor_tensor(out=lhs[:, t, own], in0=wt[:, t, own], scalar=rs2[:, t:t + 1],
                                             in1=ident, op0=ALU.mult, op1=ALU.add)
                    last = dve.tensor_scalar(lhs[:, t, other], wt[:, t, other], rs2[:, t:t + 1], None, ALU.mult)
                last.then_inc(lhs_ready, 1)
                ahead(NQ + 2)
                dve.wait_ge(bias_mm, N + 1)
                dve.tensor_copy(bias[:, wrap % 2, :], silu[:, 0:2]).then_inc(bias_ready, 1)

            count = [None]

            def period(n, wrap, products, prepares, after=True):
                if not prepares:
                    return
                N, wrap_n = n + 1, wrap + 1
                first = isinstance(n, int) and n < 0
                if first:
                    chain = [dve_step, 0, 0]
                    for q in range(AHEAD_BN):
                        bn(0, 0, 0, q, chain)
                    for q in range(AHEAD_HAAR):
                        haar(0, q, True)
                chain = [dve_step, AHEAD_BN if first else N * count[0] + AHEAD_BN, 0]
                for q in range(AHEAD_BN, NQ):
                    bn(N, wrap_n, 0, q, chain)
                layer1_in(0, chain)
                layer1_out(N, 0, chain)
                edges(N, 0, chain)
                for q in HAAR_A:
                    haar(N, q, first)
                for b in range(BLOCKS):
                    def out(before):
                        for s, where in OUT_BLOCK[b]:
                            if (where < 3 and b > 0) == before:
                                if b in SQ_DVE and s == OUT_BLOCK[b][0][0]:
                                    square(n if products else None, N, wrap_n, SQ_DVE[b], s, chain)
                                if products:
                                    empty(n, wrap, s, 1)

                    if b < BLOCKS - 1:
                        out(True)
                    dve.wait_ge(silu0_done, N * BLOCKS + (b + 1))
                    for j in range(2):
                        add_chunk(0, K_OF[2 * b + j], wrap_n, 2 * b + j, j)
                    if b % 2 == 1 and b < BLOCKS - 1:
                        edges(N, b // 2 + 1, chain)
                    if b == BLOCKS - 1:
                        layer1_in(1, chain)
                        out(True)
                        if after:
                            haar(N + 1, 0, False)
                        layer1_out(N, 1, chain)
                    out(False)
                    for i in BN1_2[b]:
                        bn(N, wrap_n, 1, i, chain)
                    for j in HAAR_2[b]:
                        haar(N, j, first)
                for i in range(NQ):
                    dve.wait_ge(silu1_done, N * NQ + (i + 1))
                    add_chunk(1, T1_ORDER[i], wrap_n, i, i % 2)
                    if i in OUT_CHUNK and products and OUT_CHUNK[i] not in ACT_CHUNK.values():
                        empty(n, wrap, OUT_CHUNK[i], 1)
                    for j in HAAR_3.get(i, ()) if after else ():
                        haar(N + 1, j, False)
                    for q in BN0_3.get(i, ()) if after else ():
                        bn(N + 1, wrap_n + 1, 0, q, chain)
                def ahead(place):
                    for q in BN0_3.get(place, ()) if after else ():
                        bn(N + 1, wrap_n + 1, 0, q, chain)

                ahead(NQ)
                layer2(N, wrap_n, chain, ahead)
                if not after:
                    return
                assert count[0] in (None, chain[2])
                count[0] = chain[2]

            period(-1, -1, False, True)
            period(0, 0, True, True)
            with dve.Fori(0, LOOPS) as turn:
                for c in range(1, UNROLL + 1):
                    period(dve.snap(turn * UNROLL + c), c, True, True)
            for n in range(LOOPS * UNROLL + 1, BATCH):
                period(n, n % UNROLL, True, n + 1 < BATCH, n + 2 < BATCH)


def constants():
    p = np.arange(P)
    ident = np.eye(P, dtype=np.float32)
    grp = (p[:, None] // GROUP == p[None, :] // GROUP) / np.float32(GROUP)
    kind = (p % ACTIVE) // KIND
    sign_h = np.where(kind % 2 == 1, -1.0, 1.0)
    sign_v = np.where(kind >= 2, -1.0, 1.0)
    signs = np.stack([np.ones(P), sign_h, sign_v, sign_h * sign_v], axis=1)
    ll4 = np.where(kind == 0, 4.0, 0.0)[:, None]
    return np.concatenate([ident, grp, signs, ll4], axis=1).astype(np.float32)


def kernel(x, L0_conv_w_ll, L0_conv_w_lh, L0_conv_w_hl, L0_conv_w_hh, L0_conv_bn_gamma, L0_conv_bn_beta,
           L0_conv_bn_mean, L0_conv_bn_var, L1_conv_P, L1_conv_mask, L1_conv_eye):
    import concourse.bacc as bacc
    from concourse.bass_utils import run_bass_kernel_spmd

    arrays = {
        "x": x,
        "P_t": np.ascontiguousarray(np.asarray(L1_conv_P).T),
        "mask_t": np.ascontiguousarray(np.asarray(L1_conv_mask).T),
        "eye_t": np.ascontiguousarray(np.asarray(L1_conv_eye).T),
        "w_ll": L0_conv_w_ll, "w_lh": L0_conv_w_lh, "w_hl": L0_conv_w_hl, "w_hh": L0_conv_w_hh,
        "gamma": L0_conv_bn_gamma, "beta": L0_conv_bn_beta, "mean": L0_conv_bn_mean, "var": L0_conv_bn_var,
        "consts": constants(),
    }
    nc = bacc.Bacc("TRN2", target_bir_lowering=False, num_devices=1, dynamic_dma_scratch_size=64)
    ins, feed = [], {}
    for name, a in arrays.items():
        a = np.ascontiguousarray(a)
        feed[f"in_{name}"] = a
        ins.append(nc.dram_tensor(f"in_{name}", a.shape, mybir.dt.from_np(a.dtype), kind="ExternalInput").ap())
    out = nc.dram_tensor("out_x2", (BATCH, CHANNELS, HEIGHT, WIDTH), F32, kind="ExternalOutput").ap()
    build(nc, *ins, out)
    r = run_bass_kernel_spmd(nc, [feed], core_ids=[0])
    return r.results[0]["out_x2"]
```
